# Optimizing a Trainium2 kernel written in Bass

```python
import numpy as np
import jax
import jax.numpy as jnp

def _softmax(x, axis=-1):
    return jax.nn.softmax(x, axis=axis)

def _gelu(x):
    return jax.nn.gelu(x, approximate=True)

def _silu(x):
    return jax.nn.silu(x)

def _sigmoid(x):
    return jax.nn.sigmoid(x)

def _layernorm(x, axis=-1, eps=1e-05):
    m = jnp.mean(x, axis=axis, keepdims=True)
    v = jnp.var(x, axis=axis, keepdims=True)
    return (x - m) / jnp.sqrt(v + eps)

def _scatter_add(tgt, idx, src, axis=0):
    return tgt.at[idx].add(src)

def _segment_sum(src, seg, n):
    return jax.ops.segment_sum(src, seg, n)
kernel_name = 'mk_adj_preln_d4_adj_r2_4ffe2e'

def setup_inputs(seed: int=0):
    np.random.seed(seed)
    _w = jnp.asarray

    def _rec_inputs():
        import jax
        import jax.numpy as jnp
        _gk = jax.random.key(seed)
        x = 7.22e-05 + 1 * jax.random.normal(jax.random.fold_in(_gk, 1), (1354, 256), jnp.float32)
        _a = jax.random.bernoulli(jax.random.fold_in(_gk, 2), 0.0118168, (1354, 1354))
        _a = jnp.logical_or(_a, jnp.swapaxes(_a, -1, -2))
        _a = jnp.logical_or(_a, jnp.eye(1354, dtype=bool))
        _af = _a.astype(jnp.float32)
        _af = _af * jax.random.uniform(jax.random.fold_in(_gk, 3), (1354, 1354), jnp.float32, 0.05, 1)
        adj = _af
        return (x, adj)
    x, adj = _rec_inputs()

    def _L0_gnn_setup():
        import jax, jax.numpy as jnp
        import numpy as np
        N = 8192
        IN_F = 256
        OUT_F = 256
        key = jax.random.key(seed)
        k1, k2, k3, k4, k5 = jax.random.split(key, 5)
        stdv = 1.0 / np.sqrt(OUT_F)
        inp = {'input': jax.random.normal(k1, (N, IN_F), dtype=jnp.float32), 'adj': jax.random.uniform(k2, (N, N), dtype=jnp.float32), 'weight': jax.random.uniform(k3, (IN_F, OUT_F), dtype=jnp.float32, minval=-stdv, maxval=stdv), 'learnable_diag_1': 0.01 * jax.random.normal(k4, (IN_F,), dtype=jnp.float32), 'bias': jax.random.uniform(k5, (OUT_F,), dtype=jnp.float32, minval=-stdv, maxval=stdv)}
        return inp
    _L0_gnn_all = _L0_gnn_setup()
    _L0_gnn_in = {k: v for k, v in _L0_gnn_all.items() if k in ('weight', 'learnable_diag_1', 'bias')}
    del _L0_gnn_all

    def _L1_gnn_setup():
        import jax, jax.numpy as jnp
        import numpy as np
        N = 3072
        D_IN = 256
        D_OUT = 256
        DENSITY = 0.005
        key = jax.random.key(seed)
        ks = jax.random.split(key, 12)
        x = jax.random.normal(ks[0], (N, D_IN), dtype=jnp.float32)
        adj_a = (jax.random.uniform(ks[1], (N, N)) < DENSITY).astype(jnp.float32)
        adj_b = (jax.random.uniform(ks[2], (N, N)) < DENSITY).astype(jnp.float32)
        W_sa = jax.random.normal(ks[3], (D_IN, D_OUT), dtype=jnp.float32) * (1.414 / np.sqrt(D_IN + D_OUT))
        a_sa = jax.random.normal(ks[4], (1, 2 * D_OUT), dtype=jnp.float32) * (1.414 / np.sqrt(1 + 2 * D_OUT))
        stdv = 1.0 / np.sqrt(D_OUT)
        W_gcnb = jax.random.uniform(ks[5], (D_IN, D_OUT), minval=-stdv, maxval=stdv, dtype=jnp.float32)
        b_gcnb = jax.random.uniform(ks[6], (D_OUT,), minval=-stdv, maxval=stdv, dtype=jnp.float32)
        s = 1.0 / np.sqrt(2 * D_IN)
        Wa = jax.random.uniform(ks[7], (1, 2 * D_IN), minval=-s, maxval=s, dtype=jnp.float32)
        ba = jax.random.uniform(ks[8], (1,), minval=-s, maxval=s, dtype=jnp.float32)
        Wb = jax.random.uniform(ks[9], (1, 2 * D_IN), minval=-s, maxval=s, dtype=jnp.float32)
        bb = jax.random.uniform(ks[10], (1,), minval=-s, maxval=s, dtype=jnp.float32)
        return {'x': x, 'adj_a': adj_a, 'adj_b': adj_b, 'W_sa': W_sa, 'a_sa': a_sa, 'W_gcnb': W_gcnb, 'b_gcnb': b_gcnb, 'Wa': Wa, 'ba': ba, 'Wb': Wb, 'bb': bb}
    _L1_gnn_all = _L1_gnn_setup()
    _L1_gnn_in = {k: v for k, v in _L1_gnn_all.items() if k in ('W_sa', 'a_sa', 'W_gcnb', 'b_gcnb', 'Wa', 'ba', 'Wb', 'bb')}
    del _L1_gnn_all

    def _L2_gnn_setup():
        import jax, jax.numpy as jnp
        import numpy as np
        N, D_IN, D_ATTN, STEPS, P_NUC, TAU = (2048, 256, 64, 2, 0.9, 1.0)
        LN_EPS = 1e-05

        def _xavier(key, shape):
            fan_in, fan_out = (shape[-2], shape[-1])
            lim = np.sqrt(6.0 / (fan_in + fan_out))
            return jax.random.uniform(key, shape, jnp.float32, -lim, lim)

        def _adj_from_feats(Xa, W1, W2, W3):
            Q = Xa @ W1
            K = Xa @ W3
            logits = Q @ W2 @ K.T / TAU
            idx = jnp.argsort(-logits, axis=1)
            vals = jnp.take_along_axis(logits, idx, axis=1)
            csum = jnp.cumsum(jax.nn.softmax(vals, axis=1), axis=1)
            k_i = jnp.sum(csum < P_NUC, axis=1) + 1
            ranks = jnp.arange(logits.shape[1])[None, :]
            keep_sorted = ranks < k_i[:, None]
            inv = jnp.argsort(idx, axis=1)
            keep = jnp.take_along_axis(keep_sorted, inv, axis=1)
            masked = jnp.where(keep, logits, -jnp.inf)
            return jax.nn.softmax(masked, axis=1)
        key = jax.random.key(seed)
        ks = jax.random.split(key, 9)
        return {'X': jax.random.normal(ks[0], (N, D_IN), jnp.float32), 'S': jax.random.uniform(ks[1], (N, N), jnp.float32), 'W1': _xavier(ks[2], (D_IN, D_ATTN)), 'W2': _xavier(ks[3], (D_ATTN, D_ATTN)), 'W3': _xavier(ks[4], (D_IN, D_ATTN)), 'U1': _xavier(ks[5], (STEPS, D_IN, D_IN)), 'U2': _xavier(ks[6], (STEPS, D_IN, D_IN)), 'U3': _xavier(ks[7], (STEPS, D_IN, D_IN)), 'gamma': jnp.ones((D_IN,), jnp.float32), 'beta': jnp.zeros((D_IN,), jnp.float32)}
    _L2_gnn_all = _L2_gnn_setup()
    _L2_gnn_in = {k: v for k, v in _L2_gnn_all.items() if k in ('W1', 'W2', 'W3', 'U1', 'U2', 'U3', 'gamma', 'beta')}
    del _L2_gnn_all

    def _L3_gnn_setup():
        import jax, jax.numpy as jnp
        import numpy as np
        N = 4096
        D_IN = 256
        D_OUT = 256
        key = jax.random.key(seed)
        k1, k2, k3, k4 = jax.random.split(key, 4)
        x = jax.random.normal(k1, (N, D_IN), dtype=jnp.float32)
        adj = jax.random.uniform(k2, (N, N), dtype=jnp.float32)
        bound = 1.0 / np.sqrt(D_IN)
        W = jax.random.uniform(k3, (D_OUT, D_IN), minval=-bound, maxval=bound, dtype=jnp.float32)
        b = jax.random.uniform(k4, (D_OUT,), minval=-bound, maxval=bound, dtype=jnp.float32)
        return {'x': x, 'adj': adj, 'W': W, 'b': b}
    _L3_gnn_all = _L3_gnn_setup()
    _L3_gnn_in = {k: v for k, v in _L3_gnn_all.items() if k in ('W', 'b')}
    del _L3_gnn_all
    return {'x': x, 'adj': adj, 'L0_gnn_weight': _L0_gnn_in['weight'], 'L0_gnn_learnable_diag_1': _L0_gnn_in['learnable_diag_1'], 'L0_gnn_bias': _L0_gnn_in['bias'], 'L1_gnn_W_sa': _L1_gnn_in['W_sa'], 'L1_gnn_a_sa': _L1_gnn_in['a_sa'], 'L1_gnn_W_gcnb': _L1_gnn_in['W_gcnb'], 'L1_gnn_b_gcnb': _L1_gnn_in['b_gcnb'], 'L1_gnn_Wa': _L1_gnn_in['Wa'], 'L1_gnn_ba': _L1_gnn_in['ba'], 'L1_gnn_Wb': _L1_gnn_in['Wb'], 'L1_gnn_bb': _L1_gnn_in['bb'], 'L2_gnn_W1': _L2_gnn_in['W1'], 'L2_gnn_W2': _L2_gnn_in['W2'], 'L2_gnn_W3': _L2_gnn_in['W3'], 'L2_gnn_U1': _L2_gnn_in['U1'], 'L2_gnn_U2': _L2_gnn_in['U2'], 'L2_gnn_U3': _L2_gnn_in['U3'], 'L2_gnn_gamma': _L2_gnn_in['gamma'], 'L2_gnn_beta': _L2_gnn_in['beta'], 'L3_gnn_W': _L3_gnn_in['W'], 'L3_gnn_b': _L3_gnn_in['b']}

def reference(x, adj, L0_gnn_weight, L0_gnn_learnable_diag_1, L0_gnn_bias, L1_gnn_W_sa, L1_gnn_a_sa, L1_gnn_W_gcnb, L1_gnn_b_gcnb, L1_gnn_Wa, L1_gnn_ba, L1_gnn_Wb, L1_gnn_bb, L2_gnn_W1, L2_gnn_W2, L2_gnn_W3, L2_gnn_U1, L2_gnn_U2, L2_gnn_U3, L2_gnn_gamma, L2_gnn_beta, L3_gnn_W, L3_gnn_b):
    import jax
    import jax.numpy as jnp

    def _L0_gnn_ref(input, adj, weight, learnable_diag_1, bias):
        import jax, jax.numpy as jnp
        import numpy as np
        N = 8192
        IN_F = 256
        OUT_F = 256
        e1 = jnp.matmul(adj, input)
        e2 = e1 * (learnable_diag_1 + 1.0)
        return jnp.matmul(input - e2, weight) + bias

    def _L1_gnn_ref(x, adj_a, adj_b, W_sa, a_sa, W_gcnb, b_gcnb, Wa, ba, Wb, bb):
        import jax, jax.numpy as jnp
        import numpy as np
        N = 3072
        D_IN = 256
        D_OUT = 256
        DENSITY = 0.005
        type_sum_a = adj_a @ x
        type_sum_b = adj_b @ x
        attn_a = jax.nn.sigmoid(jnp.concatenate([type_sum_a, x], axis=1) @ Wa.T + ba)
        attn_b = jax.nn.sigmoid(jnp.concatenate([type_sum_b, x], axis=1) @ Wb.T + bb)
        h = x @ W_sa
        Hd = h.shape[1]
        s_left = h @ a_sa[0, :Hd]
        s_right = h @ a_sa[0, Hd:]
        scores = s_left[:, None] + s_right[None, :]
        e = jnp.where(adj_a != 0, jnp.exp(-jax.nn.leaky_relu(scores, 0.01)), 0.0)
        attn = e / (jnp.sum(e, axis=1, keepdims=True) + 1e-05)
        x_a = attn @ h
        x_b = adj_b @ (x @ W_gcnb) + b_gcnb
        return jax.nn.sigmoid(attn_a * x_a + attn_b * x_b)

    def _L2_gnn_ref(X, S, W1, W2, W3, U1, U2, U3, gamma, beta):
        import jax, jax.numpy as jnp
        import numpy as np
        N, D_IN, D_ATTN, STEPS, P_NUC, TAU = (2048, 256, 64, 2, 0.9, 1.0)
        LN_EPS = 1e-05

        def _xavier(key, shape):
            fan_in, fan_out = (shape[-2], shape[-1])
            lim = np.sqrt(6.0 / (fan_in + fan_out))
            return jax.random.uniform(key, shape, jnp.float32, -lim, lim)

        def _adj_from_feats(Xa, W1, W2, W3):
            Q = Xa @ W1
            K = Xa @ W3
            logits = Q @ W2 @ K.T / TAU
            idx = jnp.argsort(-logits, axis=1)
            vals = jnp.take_along_axis(logits, idx, axis=1)
            csum = jnp.cumsum(jax.nn.softmax(vals, axis=1), axis=1)
            k_i = jnp.sum(csum < P_NUC, axis=1) + 1
            ranks = jnp.arange(logits.shape[1])[None, :]
            keep_sorted = ranks < k_i[:, None]
            inv = jnp.argsort(idx, axis=1)
            keep = jnp.take_along_axis(keep_sorted, inv, axis=1)
            masked = jnp.where(keep, logits, -jnp.inf)
            return jax.nn.softmax(masked, axis=1)
        n = X.shape[0]
        S = S + jnp.eye(n, dtype=X.dtype)
        Rf = S / jnp.clip(S.sum(axis=1, keepdims=True), 1e-12)
        Rb = S / jnp.clip(S.sum(axis=0), 1e-12)[:, None]
        Xf, Xb, Xa = (X, X, X)
        Z = jnp.zeros_like(X)
        for s in range(STEPS):
            A = _adj_from_feats(Xa, W1, W2, W3)
            Xf = Rf @ Xf
            Xb = Rb @ Xb
            Xa = A @ Xa
            Z = Z + (Xf @ U1[s] + Xb @ U2[s] + Xa @ U3[s])
        Y = X + Z
        mu = Y.mean(axis=-1, keepdims=True)
        var = Y.var(axis=-1, keepdims=True)
        return (Y - mu) / jnp.sqrt(var + LN_EPS) * gamma + beta

    def _L3_gnn_ref(x, adj, W, b):
        import jax, jax.numpy as jnp
        import numpy as np
        N = 4096
        D_IN = 256
        D_OUT = 256
        a = adj + jnp.eye(adj.shape[0], dtype=adj.dtype)
        d = jnp.sum(a, axis=1) ** (-0.5)
        a_norm = d[:, None] * a * d[None, :]
        support = a_norm @ x
        out = support @ W.T + b
        out = jax.nn.relu(out)
        return out
    h = jnp.maximum(_layernorm(x, axis=-1), 0.0)
    x = x + _L0_gnn_ref(h, adj, L0_gnn_weight, L0_gnn_learnable_diag_1, L0_gnn_bias)
    h = jnp.maximum(_layernorm(x, axis=-1), 0.0)
    x = x + _L1_gnn_ref(h, adj, adj, L1_gnn_W_sa, L1_gnn_a_sa, L1_gnn_W_gcnb, L1_gnn_b_gcnb, L1_gnn_Wa, L1_gnn_ba, L1_gnn_Wb, L1_gnn_bb)
    h = jnp.maximum(_layernorm(x, axis=-1), 0.0)
    x = x + _L2_gnn_ref(h, adj, L2_gnn_W1, L2_gnn_W2, L2_gnn_W3, L2_gnn_U1, L2_gnn_U2, L2_gnn_U3, L2_gnn_gamma, L2_gnn_beta)
    h = jnp.maximum(_layernorm(x, axis=-1), 0.0)
    x = x + _L3_gnn_ref(h, adj, L3_gnn_W, L3_gnn_b)
    return x

_drawn_inputs = setup_inputs


def setup_inputs(seed=0):
    import zlib

    import numpy as np

    out = dict(_drawn_inputs(seed))
    spreads = {'L2_gnn_gamma': (1.0, 0.2), 'L2_gnn_beta': (0.0, 0.341)}
    factors = {'L0_gnn_learnable_diag_1': 5.873,
     'L0_gnn_bias': 6.399,
     'L1_gnn_W_sa': 3.304,
     'L1_gnn_a_sa': 36.99,
     'L1_gnn_b_gcnb': 60.547,
     'L1_gnn_Wa': 64.0,
     'L1_gnn_Wb': 64.0,
     'L2_gnn_W1': 3.868,
     'L3_gnn_b': 8.0}
    for name, (base, spread) in spreads.items():
        noise = np.random.default_rng([zlib.crc32(name.encode()), seed]).standard_normal(out[name].shape)
        drawn = base * np.exp(spread * noise) if base else spread * noise
        out[name] = jnp.asarray(drawn.astype(out[name].dtype))
    for name, factor in factors.items():
        out[name] = (out[name] * factor).astype(out[name].dtype)
    return out
```

```python
from contextlib import ExitStack

import concourse.bass as bass
from concourse import mybir

P = 128
ALU = mybir.AluOpType
ACT = mybir.ActivationFunctionType
F32 = mybir.dt.float32
BF16 = mybir.dt.bfloat16
F16 = mybir.dt.float16
I32 = mybir.dt.int32
U32 = mybir.dt.uint32
AX_X = mybir.AxisListType.X
BANK = 512
LN_EPS = 1e-5
SOFT_EPS = 1e-5
SLOPE = 0.01
P_NUC = 0.9
STEPS = 2
PAIRS = (1, 5)
FULL_PROBES = 40
FIRST_PROBE = 12.0
AHEAD = 6.0
CLIP_LO, CLIP_HI = 0.04, 0.9
HUGE = 1e30


def gnn_stack(nc, x, adj, w0, diag1, bias0, w_sa, a_sa, w_gcnb, b_gcnb, wa, ba, wb, bb,
              w1, w2, w3, u1, u2, u3, gamma, beta, w_l3, b_l3, out):
    N, D = x.shape
    NT = -(-N // P)
    TAIL = N - (NT - 1) * P
    C = D // P
    A = w1.shape[1]
    GROUPS = [range(g, min(g + 4, NT)) for g in range(0, NT, 4)]
    SLICES = [(s, min(BANK, N - s)) for s in range(0, N, BANK)]
    LEAST = (1.0 - P_NUC) / N * 0.999

    def rows(t):
        return P if t < NT - 1 else TAIL

    def width(group):
        return sum(rows(t) for t in group)

    with ExitStack() as ctx:
        def sb(name, shape, dt=F32):
            return ctx.enter_context(nc.sbuf_tensor(name, shape, dt))

        def sem(name):
            return ctx.enter_context(nc.semaphore(name))

        ctx.enter_context(nc.allow_non_contiguous_dma(reason="weight columns, a few hundred words"))
        adjT = sb("adjT", [P, NT, N])
        probs = sb("probs", [P, NT, N])
        wide = sb("wide", [P, 5672])
        xres = sb("xres", [P, NT, D])
        h = sb("h", [P, NT, D])
        y = sb("y", [P, NT, D])
        hT = sb("hT", [P, C, N])
        gT = sb("gT", [P, 2 * NT * P])
        wb1 = sb("wb1", [P, C, 2 * D])
        wb2 = sb("wb2", [P, C, 2 * D + 5])
        rowv = sb("rowv", [P, 3, D])
        part = sb("part", [P, 2, D])
        w13 = sb("w13", [P, C, 2 * A])
        w2s = sb("w2s", [A, A])
        ident = sb("ident", [P, P])
        stat = sb("stat", [P, 37, NT])
        bn6 = sb("bn6", [P, 6])
        top8 = sb("top8", [P, 2, NT, 8])
        cols = sb("cols", [P, 16])
        sq32 = sb("sq32", [P, 2, 32])
        flag = sb("flag", [1, 8])
        flag_i = sb("flag_i", [1, 2], I32)
        gates = sb("gates", [P, NT, 2])
        gpre = sb("gpre", [P, NT, 3])
        ps = ctx.enter_context(nc.psum_tensor("ps", [P, 8, BANK], F32))
        psf = ps[:].rearrange("p b n -> p (b n)")
        x2_dram = nc.dram_tensor("x2_rows", (N, D), F32).ap()

        v0 = wide[:, 0:NT * (D + 2)].rearrange("p (t n) -> p t n", n=D + 2)
        hh1 = wide[:, NT * (D + 2):NT * (2 * D + 3)].rearrange("p (t n) -> p t n", n=D + 1)
        fb = wide[:, 0:NT * 2 * D].rearrange("p (t n) -> p t n", n=2 * D)
        x3 = wide[:, 0:NT * D].rearrange("p (t n) -> p t n", n=D)
        scratch = xres[:].rearrange("p t n -> p (t n)")
        masked = scratch[:, 0:N]
        qT = scratch[0:A, 0:N]
        tie = scratch[:, N:N + N // 2].bitcast(BF16)
        order = scratch[:, N + N // 2:2 * N].bitcast(F16)
        left = gT[:, 0:N]
        qwT = gT[0:A, 0:N]
        kT = gT[0:A, N:2 * N]
        sxT = gT[:, 0:C * N].rearrange("p (c n) -> p c n", c=C)
        pT = gT[:].rearrange("p (s t n) -> p s t n", s=2, t=NT)
        yflat = y[:].rearrange("p t n -> p (t n)")
        wsaT = yflat[:, 0:C * D].rearrange("p (c n) -> p c n", c=C)
        w_left = yflat[:, C * D:C * D + C * P].rearrange("p (c n) -> p c n", c=C)
        xa_row = wb2[:, 0, 0:2 * D].rearrange("p (s n) -> p s n", s=2)
        wl3 = wb2[:, 1, 0:2 * D].rearrange("p (s n) -> p s n", s=2)

        names = ("mean var std rstd shift rowsum col0 col1 col2 rinv cinv dnode zsum nmax goal least "
                 "lo mhi hi mlo probe mass reached missed s1 s2 w1 w2 f1 f2 tstar allow kept kinv above open dinv").split()
        S = {n: stat[:, i, :] for i, n in enumerate(names)}

        def pair(first):
            return stat[:, names.index(first):names.index(first) + 2, :]

        lo_mhi, hi_mlo, probe_mass, verdicts, chosen, gaps = map(pair, "lo hi probe reached s1 w1".split())

        x_in = sem("x_in")
        adj_in = [sem(f"adj_in{t}") for t in range(NT)]
        l0_in = sem("l0_in")
        l1_in = sem("l1_in")
        l2_in = sem("l2_in")
        u12_in = sem("u12_in")
        u12b_in = sem("u12b_in")
        u3_in = sem("u3_in")
        w3_in = sem("w3_in")
        vec_in = sem("vec_in")
        x2_out = sem("x2_out")
        x2_in = sem("x2_in")
        y_out = sem("y_out")
        ident_ready = sem("ident_ready")
        ones_set = sem("ones_set")
        stats_set = sem("stats_set")
        scale_ready = sem("scale_ready")
        std_ready = sem("std_ready")
        rstd_ready = sem("rstd_ready")
        h_ready = sem("h_ready")
        rows_turned = sem("rows_turned")
        hT_ready = sem("hT_ready")
        adj_turned = sem("adj_turned")
        adjT_ready = sem("adjT_ready")
        wd_ready = sem("wd_ready")
        hw_made = sem("hw_made")
        hw_taken = sem("hw_taken")
        v_made = sem("v_made")
        v_taken = sem("v_taken")
        bias_added = sem("bias_added")
        l0_made = sem("l0_made")
        l0_taken = sem("l0_taken")
        wsa_turned = sem("wsa_turned")
        wsaT_ready = sem("wsaT_ready")
        wlr_made = sem("wlr_made")
        wlr_ready = sem("wlr_ready")
        left_made = sem("left_made")
        left_ready = sem("left_ready")
        hh_made = sem("hh_made")
        hh_taken = sem("hh_taken")
        xg_made = sem("xg_made")
        xg_taken = sem("xg_taken")
        score_ready = sem("score_ready")
        leaky_ready = sem("leaky_ready")
        exp1_ready = sem("exp1_ready")
        attn_ready = sem("attn_ready")
        xb_made = sem("xb_made")
        xb_taken = sem("xb_taken")
        gates_pre = sem("gates_pre")
        gates_ready = sem("gates_ready")
        xa_made = sem("xa_made")
        mix_ready = sem("mix_ready")
        sig_ready = sem("sig_ready")
        x2_ready = sem("x2_ready")
        qk_made = sem("qk_made")
        qk_taken = sem("qk_taken")
        logits_made = sem("logits_made")
        nmax_ready = sem("nmax_ready")
        exp_ready = sem("exp_ready")
        sx_made = sem("sx_made")
        sx_taken = sem("sx_taken")
        gu_made = sem("gu_made")
        gu_taken = sem("gu_taken")
        part_ready = sem("part_ready")
        part_added = sem("part_added")
        masked_ready = sem("masked_ready")
        p_turned = sem("p_turned")
        pT_ready = sem("pT_ready")
        ax_made = sem("ax_made")
        ax_taken = sem("ax_taken")
        ax_added = sem("ax_added")
        xa_turned = sem("xa_turned")
        xaT_ready = sem("xaT_ready")
        xu_made = sem("xu_made")
        xu_taken = sem("xu_taken")
        sfb_made = sem("sfb_made")
        w3_turned = sem("w3_turned")
        w3T_ready = sem("w3T_ready")
        x2_biased = sem("x2_biased")
        norm_ready = sem("norm_ready")
        x3_ready = sem("x3_ready")
        v3_made = sem("v3_made")
        v3_taken = sem("v3_taken")
        l3_made = sem("l3_made")
        l3_taken = sem("l3_taken")
        d_ready = sem("d_ready")
        dnode_ready = sem("dnode_ready")
        out_ready = sem("out_ready")
        dve_step = sem("dve_step")
        act_step = sem("act_step")
        pool_step = sem("pool_step")
        full_step = [sem(f"full_step{s}") for s in range(STEPS)]

        class Chain:
            def __init__(self, eng, own):
                self.eng, self.own, self.counts, self.base = eng, own, {}, None

            def link(self, ins):
                n = self.counts[self.own] = self.counts.get(self.own, 0) + 1
                ins.then_inc(self.own, 1)
                self.eng.wait_ge(self.own, n if self.base is None else self.base + n)

            def tell(self, ins, other):
                n = self.counts[other] = self.counts.get(other, 0) + 1
                ins.then_inc(other, 1)
                self.eng.wait_ge(other, n)

        adj_rows = [adj[t * P:t * P + rows(t), :] for t in range(NT)]

        def row_tiles(dram):
            full = (NT - 1) * P
            return (dram[0:full, :].rearrange("(t p) d -> p t d", p=P), dram[full:N, :])

        def chunks(w):
            return w.rearrange("(c p) n -> p c n", p=P)

        def bcast(v):
            return v.partition_broadcast(P)

        block = ctx.enter_context(nc.Block())

        @block.sync
        def _(sp):
            xm, xt = row_tiles(x)
            sp.dma_start(xres[:, 0:NT - 1, :], xm).then_inc(x_in, 16)
            sp.dma_start(xres[0:TAIL, NT - 1, :], xt).then_inc(x_in, 16)
            for t in range(NT):
                sp.dma_start(probs[0:rows(t), t, :], adj_rows[t]).then_inc(adj_in[t], 16)
            sp.wait_ge(v_taken, NT)
            for k, u in enumerate((u1, u2)):
                sp.dma_start(wb1[:, :, k * D:(k + 1) * D], chunks(u[0])).then_inc(u12_in, 16)
            sp.wait_ge(hh_made, NT)
            for k, u in enumerate((u1, u2)):
                sp.dma_start(wb2[:, :, k * D:(k + 1) * D], chunks(u[1])).then_inc(u12b_in, 16)
            for t in range(NT):
                sp.wait_ge(x2_ready, t + 1)
                sp.dma_start(x2_dram[t * P:t * P + rows(t), :], xres[0:rows(t), t, :]).then_inc(x2_out, 16)
            sp.wait_ge(gu_made, 2 * NT)
            for s in range(STEPS):
                sp.dma_start(wb1[:, :, s * D:(s + 1) * D], chunks(u3[s])).then_inc(u3_in, 16)
            sp.dma_start(wl3, chunks(w_l3)).then_inc(w3_in, 16)
            sp.wait_ge(x2_ready, NT)
            for k, v in enumerate((gamma, beta, b_l3)):
                sp.dma_start(rowv[:, k, :], bcast(v)).then_inc(vec_in, 16)
            sp.wait_ge(sfb_made, NT)
            sp.wait_ge(x2_out, 16 * NT)
            xm, xt = row_tiles(x2_dram)
            sp.dma_start(x3[:, 0:NT - 1, :], xm).then_inc(x2_in, 16)
            sp.dma_start(x3[0:TAIL, NT - 1, :], xt).then_inc(x2_in, 16)
            for t in range(NT):
                sp.wait_ge(out_ready, t + 1)
                sp.dma_start(out[t * P:t * P + rows(t), :], xres[0:rows(t), t, :]).then_inc(y_out, 16)
            sp.wait_ge(y_out, 16 * NT)

        @block.gpsimd
        def _(pool):
            ch = Chain(pool, pool_step)
            ch.link(nc.gpsimd.memset(ident[:], 0.0))
            ch.tell(nc.gpsimd.affine_select(out=ident[:], in_=ident[:], compare_op=ALU.not_equal, fill=1.0,
                                            base=0, pattern=[[-1, P]], channel_multiplier=1), ident_ready)
            ch.tell(nc.gpsimd.memset(v0[:, :, D:D + 1], 1.0), ones_set)
            ch.tell(nc.gpsimd.memset(hh1[:, :, D:D + 1], 1.0), ones_set)
            pool.wait_ge(l0_in, 16 * 3)
            pool.wait_ge(h_ready, NT)
            for t in range(NT):
                r = rows(t)
                ch.tell(nc.gpsimd.tensor_tensor(xres[0:r, t, :], xres[0:r, t, :], rowv[0:r, 0, :], ALU.add),
                        bias_added)

            def add_part(n, t):
                r = rows(t)
                pool.wait_ge(part_ready, n + 1)
                ch.tell(nc.gpsimd.tensor_tensor(y[0:r, t, :], y[0:r, t, :], part[0:r, n % 2, :], ALU.add),
                        part_added)

            n = 0
            for t in range(NT):
                r = rows(t)
                add_part(n, t)
                n += 1
                ch.link(nc.gpsimd.tensor_tensor(y[0:r, t, :], y[0:r, t, :], h[0:r, t, :], ALU.add))
            for t in range(NT):
                add_part(n, t)
                n += 1
            for t in range(NT):
                for _ in range(2):
                    add_part(n, t)
                    n += 1
            pool.wait_ge(x2_in, 32)
            pool.wait_ge(vec_in, 48)
            for t in range(NT):
                r = rows(t)
                ch.tell(nc.gpsimd.tensor_tensor(x3[0:r, t, :], x3[0:r, t, :], rowv[0:r, 1, :], ALU.add),
                        x2_biased)

        @block.tensor
        def _(pe):
            def bank(b, r, n, at=0):
                return ps[0:r, b, at:at + n]

            def product(dst, pairs):
                for k, (lhsT, rhs) in enumerate(pairs):
                    last = pe.matmul(dst, lhsT, rhs, start=(k == 0), stop=(k == len(pairs) - 1))
                return last

            def turn_rows(k):
                for g, group in enumerate(GROUPS):
                    pe.wait_ge(h_ready, NT * k + group[-1] + 1)
                    for c in range(C):
                        for q, t in enumerate(group):
                            r = rows(t)
                            last = pe.transpose(bank(g * C + c, P, r, q * P), h[0:r, t, c * P:(c + 1) * P],
                                                ident[0:r, 0:r])
                        last.then_inc(rows_turned, 1)

            def adj_pairs(it, rhs, lhs=adjT, n=None):
                r = rows(it)
                return [(lhs[0:rows(jt), jt, it * P:it * P + r], rhs[0:rows(jt), jt, 0:n]) for jt in range(NT)]

            pe.wait_ge(ident_ready, 1)
            turn_rows(0)
            ring = [6, 7, 0, 1, 2, 3, 4, 5]
            n = 0
            for group in GROUPS:
                for jt in range(NT):
                    if jt == 0:
                        for t in group:
                            pe.wait_ge(adj_in[t], 16)
                    if n == 2:
                        pe.wait_ge(hT_ready, 6)
                    if n >= 8:
                        pe.wait_ge(adjT_ready, n - 7)
                    for q, t in enumerate(group):
                        r = rows(t)
                        last = pe.transpose(bank(ring[n % 8], rows(jt), r, q * P),
                                            probs[0:r, t, jt * P:jt * P + rows(jt)], ident[0:r, 0:r])
                    last.then_inc(adj_turned, 1)
                    n += 1
            pe.wait_ge(adjT_ready, n)
            pe.wait_ge(l1_in, 16 * 11)
            for e in range(C):
                for c in range(C):
                    last = pe.transpose(bank(6, P, P, e * D + c * P), wb2[:, c, e * P:(e + 1) * P], ident[:])
            last.then_inc(wsa_turned, 1)
            pe.wait_ge(wd_ready, 1)
            for t in range(NT):
                r, b = rows(t), 2 * (t % 3)
                hs = [hT[:, c, t * P:t * P + r] for c in range(C)]
                if t >= 3:
                    pe.wait_ge(hw_taken, t - 2)
                product(bank(b, r, D), [(hs[c], wb1[:, c, 0:D]) for c in range(C)]).then_inc(hw_made, 1)
                if t >= 3:
                    pe.wait_ge(v_taken, t - 2)
                product(bank(b + 1, r, D), [(hs[c], wb1[:, c, D:2 * D]) for c in range(C)]).then_inc(v_made, 1)
            pe.wait_ge(wsaT_ready, 1)
            for c in range(C):
                last = product(bank(7, P, 2, 2 * c),
                               [(wsaT[:, e, c * P:(c + 1) * P], cols[:, 2 * e:2 * e + 2]) for e in range(C)])
            last.then_inc(wlr_made, 1)
            pe.wait_ge(v_taken, NT)
            pe.wait_ge(hw_taken, NT)
            pe.wait_ge(wlr_ready, 1)
            pe.wait_ge(ones_set, 2)
            for it in range(NT):
                if it >= 8:
                    pe.wait_ge(l0_taken, it - 7)
                product(bank(it % 8, rows(it), D + 1), adj_pairs(it, v0, n=D + 1)).then_inc(l0_made, 1)

            pe.wait_ge(l0_taken, NT)
            turn_rows(1)
            pe.wait_ge(hT_ready, 12)
            for k, (s, w) in enumerate(SLICES):
                last = product(bank(5 + k, P, w), [(w_left[:, c, :], hT[:, c, s:s + w]) for c in range(C)])
            last.then_inc(left_made, 1)
            for t in range(NT):
                r, b = rows(t), 2 * (t % 2)
                hs = [hT[:, c, t * P:t * P + r] for c in range(C)]
                if t >= 2:
                    pe.wait_ge(xg_taken, t - 1)
                product(bank(b + 1, r, D + 5), [(hs[c], wb2[:, c, D:2 * D + 5]) for c in range(C)]).then_inc(xg_made, 1)
                if t >= 2:
                    pe.wait_ge(hh_taken, t - 1)
                product(bank(b, r, D), [(hs[c], wb2[:, c, 0:D]) for c in range(C)]).then_inc(hh_made, 1)
            pe.wait_ge(xg_taken, NT)
            pe.wait_ge(hh_taken, NT)
            pe.wait_ge(left_ready, 1)
            for it in range(NT):
                if it >= 8:
                    pe.wait_ge(xb_taken, it - 7)
                product(bank(it % 8, rows(it), D + 2), adj_pairs(it, v0, n=D + 2)).then_inc(xb_made, 1)
            pe.wait_ge(xb_taken, NT)
            pe.wait_ge(attn_ready, NT)
            for it in range(NT):
                if it >= 8:
                    pe.wait_ge(mix_ready, it - 7)
                product(bank(it % 8, rows(it), D + 1), adj_pairs(it, hh1, lhs=probs, n=D + 1)).then_inc(xa_made, 1)

            def logits(step):
                def project(w, src, b0):
                    for k, (s, n) in enumerate(SLICES):
                        product(bank(b0 + k, A, n),
                                [(w[:, c, :], src[:, c, s:s + n]) for c in range(C)]).then_inc(qk_made, 1)
                project(w13[:, :, 0:A], hT, 0)
                project(w13[:, :, A:2 * A], hT, 3)
                pe.wait_ge(qk_taken, 9 * step + 3)
                for k, (s, n) in enumerate(SLICES):
                    product(bank(k, A, n), [(w2s[:], qT[:, s:s + n])]).then_inc(qk_made, 1)
                pe.wait_ge(qk_taken, 9 * step + 9)
                for it in range(NT):
                    if it >= 2:
                        pe.wait_ge(exp_ready, NT * step + it - 1)
                    for k, (s, n) in enumerate(SLICES):
                        last = product(bank(4 * (it % 2) + k, rows(it), n),
                                       [(qwT[:, it * P:it * P + rows(it)], kT[:, s:s + n])])
                    last.then_inc(logits_made, 1)
                pe.wait_ge(exp_ready, NT * (step + 1))

            def weights_times(step):
                for t in range(NT):
                    r = rows(t)
                    m = step * NT + t
                    pe.wait_ge(masked_ready, m + 1)
                    for g, group in enumerate(GROUPS):
                        job = 3 * m + g
                        if job >= 6:
                            pe.wait_ge(pT_ready, job - 5)
                        for q, jt in enumerate(group):
                            last = pe.transpose(bank(job % 6, rows(jt), r, q * P),
                                                probs[0:r, t, jt * P:jt * P + rows(jt)], ident[0:r, 0:r])
                        last.then_inc(p_turned, 1)
                    pe.wait_ge(pT_ready, 3 * m + 3)
                    if m > NT:
                        pe.wait_ge(ax_added, t)
                    elif m >= 1:
                        pe.wait_ge(ax_taken, m)
                    product(bank(6, r, D), [(pT[0:rows(jt), m % 2, jt, 0:r], h[0:rows(jt), jt, :])
                                            for jt in range(NT)]).then_inc(ax_made, 1)
                    if step == 0:
                        pe.wait_ge(ax_taken, m + 1)
                        if t >= 1:
                            pe.wait_ge(xaT_ready, t)
                        for c in range(C):
                            last = pe.transpose(bank(7, P, r, c * P), xa_row[0:r, t % 2, c * P:(c + 1) * P],
                                                ident[0:r, 0:r])
                        last.then_inc(xa_turned, 1)

            pe.wait_ge(mix_ready, NT)
            pe.wait_ge(l2_in, 16 * 3)
            turn_rows(2)
            pe.wait_ge(hT_ready, 18)
            logits(0)
            for jt in range(NT):
                r = rows(jt)
                for c in range(C):
                    xs = h[0:r, jt, c * P:(c + 1) * P]
                    for k, (s, n) in enumerate(SLICES):
                        pe.matmul(bank(3 * c + k, P, n), xs, adjT[0:r, jt, s:s + n], start=(jt == 0), stop=False)
            for c in range(C):
                for k, (s, n) in enumerate(SLICES):
                    pe.matmul(bank(3 * c + k, P, n), ident[:], hT[:, c, s:s + n],
                              start=False, stop=True).then_inc(sx_made, 1)
            pe.wait_ge(u12_in, 32)
            pe.wait_ge(u12b_in, 32)
            pe.wait_ge(sx_taken, 2 * len(SLICES))
            for t in range(NT):
                r = rows(t)
                for k, w in enumerate((wb1, wb2)):
                    job = 2 * t + k
                    if t >= 2:
                        pe.wait_ge((part_ready, gu_taken)[k], t - 1)
                    product(bank(job % 4, r, 2 * D),
                            [(sxT[:, c, t * P:t * P + r], w[:, c, 0:2 * D]) for c in range(C)]).then_inc(gu_made, 1)
            pe.wait_ge(gu_taken, NT)
            weights_times(0)
            pe.wait_ge(xaT_ready, NT)
            logits(1)
            pe.wait_ge(u3_in, 32)
            for t in range(NT):
                r = rows(t)
                if t >= 4:
                    pe.wait_ge(xu_taken, t - 3)
                product(bank(t % 4, r, 2 * D),
                        [(hT[:, c, t * P:t * P + r], wb1[:, c, :]) for c in range(C)]).then_inc(xu_made, 1)
            pe.wait_ge(w3_in, 16)
            for e in range(C):
                for c in range(C):
                    last = pe.transpose(bank(4, P, P, c * D + e * P), wl3[:, e, c * P:(c + 1) * P], ident[:])
            last.then_inc(w3_turned, 1)
            pe.wait_ge(xu_taken, NT)
            pe.wait_ge(w3T_ready, 1)
            for it in range(NT):
                r = rows(it)
                if it >= 4:
                    pe.wait_ge(part_ready, 2 * NT + 2 * (it - 3))
                product(bank(it % 4, r, 2 * D), adj_pairs(it, fb, n=2 * D) +
                        [(ident[0:r, 0:r], fb[0:r, it, :])]).then_inc(sfb_made, 1)
            pe.wait_ge(part_ready, 4 * NT)
            weights_times(1)

            pe.wait_ge(ax_added, NT)
            turn_rows(3)
            pe.wait_ge(hT_ready, 24)
            for t in range(NT):
                r = rows(t)
                if t >= 8:
                    pe.wait_ge(v3_taken, t - 7)
                product(bank(t % 8, r, D), [(hT[:, c, t * P:t * P + r], wb1[:, c, 0:D]) for c in range(C)]
                        ).then_inc(v3_made, 1)
            pe.wait_ge(v3_taken, NT)
            for it in range(NT):
                r = rows(it)
                if it >= 8:
                    pe.wait_ge(l3_taken, it - 7)
                product(bank(it % 8, r, D), adj_pairs(it, y, n=D) + [(ident[0:r, 0:r], y[0:r, it, :])]
                        ).then_inc(l3_made, 1)

        @block.scalar
        def _(act):
            ch = Chain(act, act_step)
            act.dma_start(wb1[:, :, 0:D], chunks(w0)).then_inc(l0_in, 16)
            act.dma_start(cols[:, 6:6 + C], diag1.rearrange("(c p) -> p c", p=P)).then_inc(l0_in, 16)
            act.dma_start(rowv[:, 0, :], bcast(bias0)).then_inc(l0_in, 16)
            act.dma_start(wb2[:, :, 0:D], chunks(w_sa)).then_inc(l1_in, 16)
            act.dma_start(wb2[:, :, D:2 * D], chunks(w_gcnb)).then_inc(l1_in, 16)
            for k, w in enumerate((wa, wb)):
                for s in range(2):
                    act.dma_start(wb2[:, :, 2 * D + k + 2 * s],
                                  w[0, s * D:(s + 1) * D].rearrange("(c p) -> p c", p=P)).then_inc(l1_in, 16)
            for s in range(2):
                act.dma_start(cols[:, s:2 * C:2],
                              a_sa[0, s * D:(s + 1) * D].rearrange("(c p) -> p c", p=P)).then_inc(l1_in, 16)
            act.dma_start(rowv[:, 1, :], bcast(b_gcnb)).then_inc(l1_in, 16)
            act.dma_start(cols[:, 8:9], bcast(ba)).then_inc(l1_in, 16)
            act.dma_start(cols[:, 9:10], bcast(bb)).then_inc(l1_in, 16)
            act.dma_start(w13[:, :, 0:A], chunks(w1)).then_inc(l2_in, 16)
            act.dma_start(w13[:, :, A:2 * A], chunks(w3)).then_inc(l2_in, 16)
            act.dma_start(w2s[:], w2).then_inc(l2_in, 16)

            def root(k):
                act.wait_ge(scale_ready, k + 1)
                ch.tell(nc.scalar.activation(S["std"], S["var"], ACT.Sqrt, bias=cols[:, 10:11]), std_ready)

            def norm_rows(k, src):
                act.wait_ge(rstd_ready, k + 1)
                for t in range(NT):
                    r = rows(t)
                    ch.tell(nc.scalar.activation(h[0:r, t, :], src[0:r, t, :], ACT.Relu,
                                                 bias=S["shift"][0:r, t:t + 1], scale=S["rstd"][0:r, t:t + 1]),
                            h_ready)

            root(0)
            norm_rows(0, xres)
            ring = [6, 7, 0, 1, 2, 3, 4, 5]
            n = 0
            for g, group in enumerate(GROUPS):
                w = width(group)
                for jt in range(NT):
                    r = rows(jt)
                    act.wait_ge(adj_turned, n + 1)
                    ch.tell(nc.scalar.activation(adjT[0:r, jt, g * BANK:g * BANK + w], ps[0:r, ring[n % 8], 0:w],
                                                 ACT.Copy, accum_out=S[f"col{g}"][0:r, jt:jt + 1]), adjT_ready)
                    n += 1
            act.wait_ge(ones_set, 1)
            for t in range(NT):
                r = rows(t)
                act.wait_ge(v_made, t + 1)
                ch.tell(nc.scalar.copy(v0[0:r, t, 0:D], ps[0:r, 2 * (t % 3) + 1, 0:D]), v_taken)
            root(1)
            norm_rows(1, xres)
            act.wait_ge(left_made, 1)
            for k, (s, w) in enumerate(SLICES):
                ins = nc.scalar.copy(left[:, s:s + w], ps[:, 5 + k, 0:w])
                if k < len(SLICES) - 1:
                    ch.link(ins)
                else:
                    ch.tell(ins, left_ready)
            for t in range(NT):
                r = rows(t)
                act.wait_ge(hh_made, t + 1)
                ch.tell(nc.scalar.copy(hh1[0:r, t, 0:D], ps[0:r, 2 * (t % 2), 0:D]), hh_taken)
            act.wait_ge(xg_taken, NT)
            for t in range(NT):
                r = rows(t)
                ch.tell(nc.scalar.activation(probs[0:r, t, :], left[0:r, :], ACT.Identity,
                                             bias=gpre[0:r, t, 2:3]), score_ready)
            for t in range(NT):
                r = rows(t)
                act.wait_ge(leaky_ready, t + 1)
                ch.tell(nc.scalar.activation(probs[0:r, t, :], probs[0:r, t, :], ACT.Exp, scale=-1.0), exp1_ready)
            act.wait_ge(gates_pre, 1)
            ch.tell(nc.scalar.activation(gates[:], gates[:], ACT.Sigmoid), gates_ready)
            for t in range(NT):
                r = rows(t)
                act.wait_ge(mix_ready, t + 1)
                ch.tell(nc.scalar.activation(y[0:r, t, :], y[0:r, t, :], ACT.Sigmoid), sig_ready)
            root(2)
            norm_rows(2, xres)

            def softmax_rows(step):
                for t in range(NT):
                    r = rows(t)
                    b = 4 * (t % 2) * BANK
                    act.wait_ge(nmax_ready, NT * step + t + 1)
                    ch.tell(nc.scalar.activation(probs[0:r, t, :], psf[0:r, b:b + N], ACT.Exp,
                                                 bias=S["nmax"][0:r, t:t + 1],
                                                 accum_out=S["zsum"][0:r, t:t + 1]), exp_ready)

            parts = [0]

            def part_out(src, scale, r):
                n = parts[0]
                if n >= 2:
                    act.wait_ge(part_added, n - 1)
                ins = nc.scalar.activation(part[0:r, n % 2, :], src, ACT.Copy, scale=scale)
                parts[0] += 1
                return ins

            def turned_weights(step, t):
                r = rows(t)
                m = step * NT + t
                for g, group in enumerate(GROUPS):
                    job = 3 * m + g
                    act.wait_ge(p_turned, job + 1)
                    if m >= 2 and g == 0:
                        act.wait_ge(ax_made, m - 1)
                    full = [jt for jt in group if rows(jt) == P]
                    k = len(full)
                    src = ps[:, job % 6, 0:k * P].rearrange("p (q n) -> p q n", n=P)[:, :, 0:r]
                    ins = nc.scalar.copy(pT[:, m % 2, group[0]:group[0] + k, 0:r], src)
                    if k == len(group):
                        ch.tell(ins, pT_ready)
                    else:
                        ch.link(ins)
                        jt = group[-1]
                        ch.tell(nc.scalar.copy(pT[0:rows(jt), m % 2, jt, 0:r],
                                               ps[0:rows(jt), job % 6, k * P:k * P + r]), pT_ready)

            softmax_rows(0)
            for c in range(C):
                for k, (s, n) in enumerate(SLICES):
                    act.wait_ge(sx_made, 3 * c + k + 1)
                    ch.tell(nc.scalar.copy(sxT[:, c, s:s + n], ps[:, 3 * c + k, 0:n]), sx_taken)
            for t in range(NT):
                r = rows(t)
                dr, dc = S["rinv"][0:r, t:t + 1], S["cinv"][0:r, t:t + 1]
                act.wait_ge(gu_made, 2 * t + 1)
                b = (2 * t) % 4
                ch.link(nc.scalar.activation(y[0:r, t, :], ps[0:r, b, 0:D], ACT.Copy, scale=dr))
                ch.tell(part_out(ps[0:r, b, D:2 * D], dc, r), part_ready)
                act.wait_ge(gu_made, 2 * t + 2)
                ch.link(nc.scalar.activation(fb[0:r, t, 0:D], ps[0:r, b + 1, 0:D], ACT.Copy, scale=dr))
                ch.tell(nc.scalar.activation(fb[0:r, t, D:2 * D], ps[0:r, b + 1, D:2 * D], ACT.Copy, scale=dc),
                        gu_taken)
            for t in range(NT):
                r = rows(t)
                turned_weights(0, t)
                act.wait_ge(ax_made, t + 1)
                if t >= 2:
                    act.wait_ge(xa_turned, t - 1)
                ch.tell(nc.scalar.activation(xa_row[0:r, t % 2, :], ps[0:r, 6, 0:D], ACT.Copy,
                                             scale=S["kinv"][0:r, t:t + 1]), ax_taken)
                act.wait_ge(xa_turned, t + 1)
                ch.tell(nc.scalar.copy(hT[:, :, t * P:t * P + r],
                                       ps[:, 7, 0:C * P].rearrange("p (c n) -> p c n", c=C)[:, :, 0:r]), xaT_ready)
            softmax_rows(1)
            for t in range(NT):
                r = rows(t)
                act.wait_ge(xu_made, t + 1)
                ch.tell(part_out(ps[0:r, t % 4, 0:D], 1.0, r), part_ready)
                ch.tell(nc.scalar.copy(h[0:r, t, :], ps[0:r, t % 4, D:2 * D]), xu_taken)
            act.wait_ge(w3_turned, 1)
            act.wait_ge(xu_made, NT)
            ch.tell(nc.scalar.copy(wb1[:, :, 0:D], ps[:, 4, :].rearrange("p (c n) -> p c n", c=C)), w3T_ready)
            for t in range(NT):
                r = rows(t)
                dr, dc = S["rinv"][0:r, t:t + 1], S["cinv"][0:r, t:t + 1]
                act.wait_ge(sfb_made, t + 1)
                ch.tell(part_out(ps[0:r, t % 4, 0:D], dr, r), part_ready)
                ch.tell(part_out(ps[0:r, t % 4, D:2 * D], dc, r), part_ready)
            for t in range(NT):
                turned_weights(1, t)
            root(3)
            act.wait_ge(rstd_ready, 4)
            for t in range(NT):
                r = rows(t)
                ch.tell(nc.scalar.activation(y[0:r, t, :], y[0:r, t, :], ACT.Identity,
                                             bias=S["shift"][0:r, t:t + 1], scale=S["rstd"][0:r, t:t + 1]),
                        norm_ready)
            act.wait_ge(d_ready, 1)
            ch.tell(nc.scalar.activation(S["dnode"], S["dinv"], ACT.Sqrt), dnode_ready)
            root(4)
            act.wait_ge(rstd_ready, 5)
            for t in range(NT):
                r = rows(t)
                ch.tell(nc.scalar.activation(h[0:r, t, :], x3[0:r, t, :], ACT.Relu,
                                             bias=S["shift"][0:r, t:t + 1], scale=S["rstd"][0:r, t:t + 1]),
                        h_ready)

        @block.vector
        def _(dve):
            ch = Chain(dve, dve_step)
            V = nc.vector
            ch.link(V.memset(stat[:], 1.0))
            ch.link(V.memset(top8[:], 1.0))
            ch.link(V.memset(gates[:], 0.0))
            ch.link(V.memset(gpre[:], 0.0))
            ch.link(V.memset(cols[:, 10:11], LN_EPS))
            ch.link(V.memset(sq32[:], 0.0))

            def stats_of(src, t):
                r = rows(t)
                ch.link(V.bn_stats(bn6[0:r, :], src))
                aggr = V.bn_aggr(stat[0:r, 0:2, t], bn6[0:r, :])
                if t < NT - 1:
                    ch.link(aggr)
                else:
                    ch.tell(aggr, scale_ready)

            def scales(k):
                dve.wait_ge(std_ready, k + 1)
                ch.link(V.reciprocal(S["rstd"], S["std"]))
                ch.tell(V.scalar_tensor_tensor(S["shift"], S["mean"], -1.0, S["rstd"], ALU.mult, ALU.mult),
                        rstd_ready)

            def take_turned(k):
                for g, group in enumerate(GROUPS):
                    w = width(group)
                    for c in range(C):
                        dve.wait_ge(rows_turned, 6 * k + g * C + c + 1)
                        ch.tell(V.tensor_copy(hT[:, c, g * BANK:g * BANK + w], ps[:, g * C + c, 0:w]), hT_ready)

            dve.wait_ge(x_in, 32)
            for t in range(NT):
                stats_of(xres[0:rows(t), t, :], t)
            scales(0)
            dve.wait_ge(l0_in, 16 * 3)
            ch.link(V.tensor_scalar(cols[:, 6:6 + C], cols[:, 6:6 + C], 1.0, None, ALU.add))
            for c in range(C):
                ins = V.tensor_scalar(wb1[:, c, D:2 * D], wb1[:, c, 0:D], cols[:, 6 + c:7 + c], None, ALU.mult)
                if c < C - 1:
                    ch.link(ins)
                else:
                    ch.tell(ins, wd_ready)
            take_turned(0)
            dve.wait_ge(wsa_turned, 1)
            ch.tell(V.tensor_copy(wsaT, ps[:, 6, :].rearrange("p (c n) -> p c n", c=C)), wsaT_ready)
            for t in range(NT):
                r = rows(t)
                dve.wait_ge(hw_made, t + 1)
                dve.wait_ge(bias_added, t + 1)
                ch.tell(V.tensor_tensor(xres[0:r, t, :], xres[0:r, t, :], ps[0:r, 2 * (t % 3), 0:D], ALU.add),
                        hw_taken)
            dve.wait_ge(wlr_made, 1)
            for c in range(C):
                ch.link(V.memset(w_left[:, c, :], 1.0))
                ch.link(V.tensor_scalar(w_left[:, c, :], w_left[:, c, :], ps[:, 7, 2 * c:2 * c + 1], None, ALU.mult))
                ins = V.tensor_copy(wb2[:, c, 2 * D + 4:2 * D + 5], ps[:, 7, 2 * c + 1:2 * c + 2])
                if c < C - 1:
                    ch.link(ins)
                else:
                    ch.tell(ins, wlr_ready)
            for t in range(NT):
                r = rows(t)
                dve.wait_ge(l0_made, t + 1)
                ch.link(V.tensor_tensor(xres[0:r, t, :], xres[0:r, t, :], ps[0:r, t % 8, 0:D], ALU.subtract))
                ch.tell(V.tensor_copy(S["rowsum"][0:r, t:t + 1], ps[0:r, t % 8, D:D + 1]), l0_taken)
                stats_of(xres[0:r, t, :], t)
            scales(1)
            ch.link(V.tensor_scalar(S["rinv"], S["rowsum"], 1.0, 1e-12, ALU.add, ALU.max))
            ch.link(V.reciprocal(S["rinv"], S["rinv"]))
            ch.link(V.tensor_tensor(S["cinv"], S["col0"], S["col1"], ALU.add))
            ch.link(V.tensor_tensor(S["cinv"], S["cinv"], S["col2"], ALU.add))
            ch.link(V.tensor_scalar(S["cinv"], S["cinv"], 1.0, 1e-12, ALU.add, ALU.max))
            ch.link(V.reciprocal(S["cinv"], S["cinv"]))
            ch.link(V.tensor_scalar(S["dinv"], S["rowsum"], 1.0, None, ALU.add))
            ch.tell(V.reciprocal(S["dinv"], S["dinv"]), d_ready)
            take_turned(1)
            dve.wait_ge(l1_in, 16 * 11)
            for t in range(NT):
                r = rows(t)
                dve.wait_ge(xg_made, t + 1)
                b = 2 * (t % 2) + 1
                ch.link(V.tensor_copy(v0[0:r, t, :], ps[0:r, b, 0:D + 2]))
                ch.tell(V.tensor_copy(gpre[0:r, t, :], ps[0:r, b, D + 2:D + 5]), xg_taken)
            for t in range(NT):
                row = probs[0:rows(t), t, :]
                dve.wait_ge(score_ready, t + 1)
                ch.tell(V.scalar_tensor_tensor(row, row, SLOPE, row, ALU.mult, ALU.max), leaky_ready)
            for t in range(NT):
                r = rows(t)
                dve.wait_ge(exp1_ready, t + 1)
                ch.tell(V.scalar_tensor_tensor(probs[0:r, t, :], adjT[0:r, t, :], 0.0, probs[0:r, t, :],
                                               ALU.not_equal, ALU.mult), attn_ready)
            for t in range(NT):
                r = rows(t)
                dve.wait_ge(xb_made, t + 1)
                ch.link(V.tensor_tensor(y[0:r, t, :], ps[0:r, t % 8, 0:D], rowv[0:r, 1, :], ALU.add))
                ch.tell(V.tensor_tensor(gates[0:r, t, :], ps[0:r, t % 8, D:D + 2], gpre[0:r, t, 0:2], ALU.add),
                        xb_taken)
            ch.link(V.tensor_scalar(gates[:, :, 0], gates[:, :, 0], cols[:, 8:9], None, ALU.add))
            ch.tell(V.tensor_scalar(gates[:, :, 1], gates[:, :, 1], cols[:, 9:10], None, ALU.add), gates_pre)
            dve.wait_ge(gates_ready, 1)

            def mix(t):
                r = rows(t)
                dve.wait_ge(xa_made, t + 1)
                ratio = S["f1"][0:r, t:t + 1]
                ch.link(V.tensor_scalar(ratio, ps[0:r, t % 8, D:D + 1], SOFT_EPS, None, ALU.add))
                ch.link(V.reciprocal(ratio, ratio))
                ch.link(V.tensor_tensor(ratio, ratio, gates[0:r, t, 0:1], ALU.mult))
                ch.link(V.tensor_scalar(y[0:r, t, :], y[0:r, t, :], gates[0:r, t, 1:2], None, ALU.mult))
                ch.tell(V.scalar_tensor_tensor(y[0:r, t, :], ps[0:r, t % 8, 0:D], ratio, y[0:r, t, :],
                                               ALU.mult, ALU.add), mix_ready)

            def residual(t):
                r = rows(t)
                dve.wait_ge(sig_ready, t + 1)
                ch.tell(V.tensor_tensor(xres[0:r, t, :], xres[0:r, t, :], y[0:r, t, :], ALU.add), x2_ready)
                stats_of(xres[0:r, t, :], t)

            for t in range(NT + 1):
                if t < NT:
                    mix(t)
                if t >= 1:
                    residual(t - 1)
            scales(2)
            take_turned(2)
            dve.wait_ge(x2_out, 16 * NT)

            def project_out(step):
                for k in range(9):
                    s, n = SLICES[k % 3]
                    dst = (qT, kT, qwT)[k // 3]
                    b = k if k < 6 else k - 6
                    dve.wait_ge(qk_made, 9 * step + k + 1)
                    ch.tell(V.tensor_copy(dst[:, s:s + n], ps[0:A, b, 0:n]), qk_taken)

            def maxima(step):
                for t in range(NT):
                    r = rows(t)
                    b = 4 * (t % 2) * BANK
                    dve.wait_ge(logits_made, NT * step + t + 1)
                    ch.tell(V.tensor_reduce(S["nmax"][0:r, t:t + 1], psf[0:r, b:b + N], AX_X, ALU.max, negate=True),
                            nmax_ready)

            def mass_above(c, limit, mass):
                for t in range(NT):
                    r = rows(t)
                    c.link(V.scalar_tensor_tensor(masked[0:r, :], probs[0:r, t, :], limit[0:r, t:t + 1],
                                                  probs[0:r, t, :], ALU.is_ge, ALU.mult,
                                                  accum_out=mass[0:r, t:t + 1]))

            def narrow(c):
                mass_above(c, S["probe"], S["mass"])
                c.link(V.tensor_tensor(S["reached"], S["mass"], S["goal"], ALU.is_ge))
                c.link(V.tensor_tensor(S["missed"], S["mass"], S["goal"], ALU.is_lt))
                c.link(V.tensor_tensor(chosen, probe_mass, verdicts, ALU.mult))
                c.link(V.tensor_tensor(lo_mhi, lo_mhi, chosen, ALU.max))
                c.link(V.scalar_tensor_tensor(chosen, verdicts, HUGE, probe_mass, ALU.mult, ALU.max))
                c.link(V.tensor_tensor(hi_mlo, hi_mlo, chosen, ALU.min))

            def midpoint(c):
                c.link(V.tensor_tensor(S["w1"], S["hi"], S["lo"], ALU.subtract))
                c.link(V.scalar_tensor_tensor(S["probe"], S["w1"], 0.5, S["lo"], ALU.mult, ALU.add))

            def interpolate(c):
                c.link(V.tensor_tensor(gaps, hi_mlo, lo_mhi, ALU.subtract))
                c.link(V.scalar_tensor_tensor(S["f1"], S["lo"], AHEAD, S["mlo"], ALU.mult, ALU.add))
                c.link(V.tensor_tensor(S["f1"], S["f1"], S["goal"], ALU.subtract))
                c.link(V.reciprocal(S["f2"], S["w2"]))
                c.link(V.tensor_tensor(S["f1"], S["f1"], S["f2"], ALU.mult))
                c.link(V.tensor_scalar(S["f1"], S["f1"], CLIP_LO, CLIP_HI, ALU.max, ALU.min))
                c.link(V.tensor_tensor(S["f1"], S["f1"], S["w1"], ALU.mult))
                c.link(V.tensor_tensor(S["probe"], S["lo"], S["f1"], ALU.add))

            def threshold(c):
                for t in range(NT):
                    r = rows(t)
                    c.link(V.scalar_tensor_tensor(masked[0:r, :], probs[0:r, t, :], S["hi"][0:r, t:t + 1],
                                                  probs[0:r, t, :], ALU.is_lt, ALU.mult))
                    c.link(V.max(top8[0:r, 0, t, :], masked[0:r, :]))
                vals, sums = top8[:, 0, :, :], top8[:, 1, :, :]
                c.link(V.tensor_tensor(sums[:, :, 0], vals[:, :, 0], S["mhi"], ALU.add))
                for k in range(1, 8):
                    c.link(V.tensor_tensor(sums[:, :, k], sums[:, :, k - 1], vals[:, :, k], ALU.add))
                goal8 = S["goal"].unsqueeze(2).broadcast_to([P, NT, 8])
                c.link(V.tensor_tensor(sums, sums, goal8, ALU.is_ge))
                c.link(V.tensor_tensor(sums, sums, vals, ALU.mult))
                c.link(V.tensor_reduce(S["tstar"], sums, AX_X, ALU.max))
                c.link(V.tensor_tensor(S["tstar"], S["tstar"], vals[:, :, 7], ALU.max))
                t8 = S["tstar"].unsqueeze(2).broadcast_to([P, NT, 8])
                c.link(V.tensor_tensor(sums, vals, t8, ALU.is_gt))
                c.link(V.tensor_tensor(sums, sums, vals, ALU.mult))
                c.link(V.tensor_reduce(S["above"], sums, AX_X, ALU.add))
                c.link(V.tensor_tensor(S["above"], S["above"], S["mhi"], ALU.add))
                c.link(V.tensor_tensor(S["allow"], S["goal"], S["above"], ALU.subtract))
                c.link(V.reciprocal(S["f1"], S["tstar"]))
                c.link(V.tensor_tensor(S["allow"], S["allow"], S["f1"], ALU.mult))
                c.link(V.tensor_scalar(S["allow"], S["allow"], 1.0, None, ALU.add))

            PROBE = NT + 6
            PAIR = 2 * PROBE + 2 + 8

            def search(step):
                ch.link(V.tensor_scalar(S["goal"], S["zsum"], P_NUC, None, ALU.mult))
                ch.link(V.tensor_scalar(S["lo"], S["zsum"], LEAST, None, ALU.mult))
                ch.link(V.tensor_copy(S["mlo"], S["zsum"]))
                ch.link(V.memset(S["hi"], 1.5))
                ch.link(V.memset(S["mhi"], 0.0))
                ch.link(V.tensor_scalar(S["probe"], S["lo"], FIRST_PROBE, 0.75, ALU.mult, ALU.min))
                narrow(ch)
                base = ch.counts[dve_step]
                with dve.Fori(0, PAIRS[step]) as i:
                    ch.counts[dve_step] = 0
                    ch.base = i * PAIR + base
                    midpoint(ch)
                    narrow(ch)
                    interpolate(ch)
                    narrow(ch)
                    assert ch.counts[dve_step] == PAIR
                ch.base = None
                ch.counts[dve_step] = base + PAIR * PAIRS[step]
                threshold(ch)
                mass_above(ch, S["tstar"], S["mass"])
                ch.link(V.tensor_tensor(S["open"], S["mass"], S["goal"], ALU.is_lt))
                ch.link(V.tensor_reduce(sq32[:, 0, 0:1], S["open"], AX_X, ALU.max))
                ch.link(V.transpose(sq32[:, 1, :], sq32[:, 0, :]))
                ch.link(V.tensor_reduce(cols[:, 12:13], sq32[:, 1, :], AX_X, ALU.max))
                for q in range(4):
                    ch.link(V.tensor_copy(flag[:, q:q + 1], cols[32 * q:32 * q + 1, 12:13]))
                ch.link(V.tensor_reduce(flag[:, 4:5], flag[:, 0:4], AX_X, ALU.max))
                ch.link(V.tensor_copy(flag_i[:, 0:1], flag[:, 4:5]))
                any_open = dve.value_load(flag_i[0:1, 0:1], min_val=0, max_val=1)
                with dve.If(any_open > 0):
                    full = Chain(dve, full_step[step])
                    with dve.Fori(0, FULL_PROBES) as i:
                        full.base = i * (PROBE + 2)
                        midpoint(full)
                        narrow(full)
                    full.base = None
                    full.counts[full_step[step]] = FULL_PROBES * (PROBE + 2)
                    threshold(full)

            def keep(step, t):
                r = rows(t)
                row, ts = probs[0:r, t, :], S["tstar"][0:r, t:t + 1]
                ch.link(V.scalar_tensor_tensor(masked[0:r, :], row, ts, row, ALU.is_gt, ALU.mult))
                ch.link(V.tensor_scalar(tie[0:r, :], row, ts, None, ALU.is_equal))
                ch.link(V.tensor_tensor_scan(order[0:r, :], tie[0:r, :], tie[0:r, :], 0.0, ALU.add, ALU.max))
                ch.link(V.scalar_tensor_tensor(tie[0:r, :], order[0:r, :], S["allow"][0:r, t:t + 1], tie[0:r, :],
                                               ALU.is_lt, ALU.mult))
                ch.link(V.scalar_tensor_tensor(row, tie[0:r, :], ts, masked[0:r, :], ALU.mult, ALU.add,
                                               accum_out=S["kept"][0:r, t:t + 1]))
                ch.tell(V.reciprocal(S["kinv"][0:r, t:t + 1], S["kept"][0:r, t:t + 1]), masked_ready)

            project_out(0)
            maxima(0)
            dve.wait_ge(exp_ready, NT)
            search(0)
            for t in range(NT):
                keep(0, t)
            project_out(1)
            maxima(1)
            dve.wait_ge(exp_ready, 2 * NT)
            search(1)
            dve.wait_ge(part_added, 4 * NT)
            for t in range(NT + 1):
                if t < NT:
                    keep(1, t)
                if t >= 1:
                    r = rows(t - 1)
                    dve.wait_ge(ax_made, NT + t)
                    row = y[0:r, t - 1, :]
                    ch.tell(V.scalar_tensor_tensor(row, ps[0:r, 6, 0:D], S["kinv"][0:r, t - 1:t], row,
                                                   ALU.mult, ALU.add), ax_added)
                    stats_of(row, t - 1)
            scales(3)
            dve.wait_ge(vec_in, 48)
            for t in range(NT):
                r = rows(t)
                dve.wait_ge(norm_ready, t + 1)
                ch.link(V.tensor_tensor(y[0:r, t, :], y[0:r, t, :], rowv[0:r, 0, :], ALU.mult))
                dve.wait_ge(x2_biased, t + 1)
                ch.link(V.tensor_tensor(x3[0:r, t, :], x3[0:r, t, :], y[0:r, t, :], ALU.add))
                stats_of(x3[0:r, t, :], t)
            scales(4)
            take_turned(3)
            dve.wait_ge(dnode_ready, 1)
            for t in range(NT):
                r = rows(t)
                dve.wait_ge(v3_made, t + 1)
                ch.tell(V.tensor_scalar(y[0:r, t, :], ps[0:r, t % 8, 0:D], S["dnode"][0:r, t:t + 1], None,
                                        ALU.mult), v3_taken)
            for t in range(NT):
                r = rows(t)
                dve.wait_ge(l3_made, t + 1)
                o = xres[0:r, t, :]
                ch.tell(V.scalar_tensor_tensor(o, ps[0:r, t % 8, 0:D], S["dnode"][0:r, t:t + 1], rowv[0:r, 2, :],
                                               ALU.mult, ALU.add), l3_taken)
                ch.tell(V.scalar_tensor_tensor(o, o, 0.0, x3[0:r, t, :], ALU.max, ALU.add), out_ready)


INS = ("x", "adj", "L0_gnn_weight", "L0_gnn_learnable_diag_1", "L0_gnn_bias", "L1_gnn_W_sa", "L1_gnn_a_sa",
       "L1_gnn_W_gcnb", "L1_gnn_b_gcnb", "L1_gnn_Wa", "L1_gnn_ba", "L1_gnn_Wb", "L1_gnn_bb", "L2_gnn_W1",
       "L2_gnn_W2", "L2_gnn_W3", "L2_gnn_U1", "L2_gnn_U2", "L2_gnn_U3", "L2_gnn_gamma", "L2_gnn_beta",
       "L3_gnn_W", "L3_gnn_b")


def kernel(**inputs):
    import numpy as np
    import concourse.bacc as bacc
    from concourse.bass_utils import run_bass_kernel_spmd

    nc = bacc.Bacc("TRN2", target_bir_lowering=False, num_devices=1, dynamic_dma_scratch_size=4096)
    arrays, args = {}, []
    for name in INS:
        a = np.ascontiguousarray(inputs[name])
        arrays[f"in_{name}"] = a
        args.append(nc.dram_tensor(f"in_{name}", a.shape, mybir.dt.from_np(a.dtype), kind="ExternalInput").ap())
    out = nc.dram_tensor("out_rows", inputs["x"].shape, F32, kind="ExternalOutput").ap()
    gnn_stack(nc, *args, out)
    result = run_bass_kernel_spmd(nc, [arrays], core_ids=[0])
    return result.results[0]["out_rows"]
```

```python
from contextlib import ExitStack

import concourse.bass as bass
from concourse import mybir

P = 128
ALU = mybir.AluOpType
ACT = mybir.ActivationFunctionType
F32 = mybir.dt.float32
BF16 = mybir.dt.bfloat16
F16 = mybir.dt.float16
I32 = mybir.dt.int32
U32 = mybir.dt.uint32
AX_X = mybir.AxisListType.X
BANK = 512
LN_EPS = 1e-5
SOFT_EPS = 1e-5
SLOPE = 0.01
P_NUC = 0.9
STEPS = 2
PAIRS = (1, 6)
MORE_PAIRS = 2
SHARED = 3
BELOW = 1.0 - 2.0 ** -24
FULL_PROBES = 40
FIRST_PROBE = 12.0
AHEAD = 6.0
CLIP_LO, CLIP_HI = 0.04, 0.9
HUGE = 1e30


def gnn_stack(nc, x, adj, w0, diag1, bias0, w_sa, a_sa, w_gcnb, b_gcnb, wa, ba, wb, bb,
              w1, w2, w3, u1, u2, u3, gamma, beta, w_l3, b_l3, out):
    N, D = x.shape
    NT = -(-N // P)
    TAIL = N - (NT - 1) * P
    C = D // P
    A = w1.shape[1]
    GROUPS = [range(g, min(g + 4, NT)) for g in range(0, NT, 4)]
    SLICES = [(s, min(BANK, N - s)) for s in range(0, N, BANK)]
    LEAST = (1.0 - P_NUC) / N * 0.999

    def rows(t):
        return P if t < NT - 1 else TAIL

    def width(group):
        return sum(rows(t) for t in group)

    with ExitStack() as ctx:
        def sb(name, shape, dt=F32):
            return ctx.enter_context(nc.sbuf_tensor(name, shape, dt))

        def sem(name):
            return ctx.enter_context(nc.semaphore(name))

        ctx.enter_context(nc.allow_non_contiguous_dma(reason="weight columns, a few hundred words"))
        adjT = sb("adjT", [P, NT, N])
        probs = sb("probs", [P, NT, N])
        wide = sb("wide", [P, 5672])
        xres = sb("xres", [P, NT, D])
        h = sb("h", [P, NT, D])
        y = sb("y", [P, NT, D])
        hT = sb("hT", [P, C, N])
        gT = sb("gT", [P, 2 * NT * P])
        wb1 = sb("wb1", [P, C, 2 * D])
        wb2 = sb("wb2", [P, C, 2 * D + 5])
        rowv = sb("rowv", [P, 3, D])
        part = sb("part", [P, 2, D])
        w13 = sb("w13", [P, C, 2 * A])
        w2s = sb("w2s", [A, A])
        ident = sb("ident", [P, P])
        waste = sb("waste", [P, N], BF16)
        stat = sb("stat", [P, 41, NT])
        bn6 = sb("bn6", [P, 6])
        top8 = sb("top8", [P, 2, NT, 8])
        cols = sb("cols", [P, 16])
        sq32 = sb("sq32", [P, 2, 32])
        flag = sb("flag", [1, 8])
        flag_i = sb("flag_i", [1, 2], I32)
        gates = sb("gates", [P, NT, 2])
        gpre = sb("gpre", [P, NT, 3])
        ps = ctx.enter_context(nc.psum_tensor("ps", [P, 8, BANK], F32))
        psf = ps[:].rearrange("p b n -> p (b n)")
        x2_dram = nc.dram_tensor("x2_rows", (N, D), F32).ap()

        v0 = wide[:, 0:NT * (D + 2)].rearrange("p (t n) -> p t n", n=D + 2)
        hh1 = wide[:, NT * (D + 2):NT * (2 * D + 3)].rearrange("p (t n) -> p t n", n=D + 1)
        fb = wide[:, 0:NT * 2 * D].rearrange("p (t n) -> p t n", n=2 * D)
        x3 = wide[:, 0:NT * D].rearrange("p (t n) -> p t n", n=D)
        scratch = xres[:].rearrange("p t n -> p (t n)")
        masked = scratch[:, 0:N]
        qT = scratch[0:A, 0:N]
        tie = scratch[:, N:N + N // 2].bitcast(BF16)
        order = scratch[:, N + N // 2:2 * N].bitcast(F16)
        left = gT[:, 0:N]
        qwT = gT[0:A, 0:N]
        kT = gT[0:A, N:2 * N]
        sxT = gT[:, 0:C * N].rearrange("p (c n) -> p c n", c=C)
        pT = gT[:].rearrange("p (s t n) -> p s t n", s=2, t=NT)
        yflat = y[:].rearrange("p t n -> p (t n)")
        wsaT = yflat[:, 0:C * D].rearrange("p (c n) -> p c n", c=C)
        w_left = yflat[:, C * D:C * D + C * P].rearrange("p (c n) -> p c n", c=C)
        xa_row = wb2[:, 0, 0:2 * D].rearrange("p (s n) -> p s n", s=2)
        wl3 = wb2[:, 1, 0:2 * D].rearrange("p (s n) -> p s n", s=2)

        names = ("mean var std rstd shift rowsum col0 col1 col2 rinv cinv dnode zsum nmax goal least "
                 "lo mhi hi mlo probe mass reached missed s1 s2 w1 w2 f1 f2 tstar allow kept kinv above open dinv "
                 "spred ssum scount partial").split()
        S = {n: stat[:, i, :] for i, n in enumerate(names)}

        def pair(first):
            return stat[:, names.index(first):names.index(first) + 2, :]

        lo_mhi, hi_mlo, probe_mass, verdicts, chosen, gaps = map(pair, "lo hi probe reached s1 w1".split())

        x_in = sem("x_in")
        adj_in = [sem(f"adj_in{t}") for t in range(NT)]
        l0_in = sem("l0_in")
        l1_in = sem("l1_in")
        l2_in = sem("l2_in")
        u12_in = sem("u12_in")
        u12b_in = sem("u12b_in")
        u3_in = sem("u3_in")
        w3_in = sem("w3_in")
        vec_in = sem("vec_in")
        x2_out = sem("x2_out")
        x2_in = sem("x2_in")
        y_out = sem("y_out")
        ident_ready = sem("ident_ready")
        ones_set = sem("ones_set")
        stats_set = sem("stats_set")
        scale_ready = sem("scale_ready")
        std_ready = sem("std_ready")
        rstd_ready = sem("rstd_ready")
        h_ready = sem("h_ready")
        rows_turned = sem("rows_turned")
        hT_ready = sem("hT_ready")
        adj_turned = sem("adj_turned")
        adjT_ready = sem("adjT_ready")
        wd_ready = sem("wd_ready")
        hw_made = sem("hw_made")
        hw_taken = sem("hw_taken")
        v_made = sem("v_made")
        v_taken = sem("v_taken")
        bias_added = sem("bias_added")
        l0_made = sem("l0_made")
        l0_taken = sem("l0_taken")
        wsa_turned = sem("wsa_turned")
        wsaT_ready = sem("wsaT_ready")
        wlr_made = sem("wlr_made")
        wlr_ready = sem("wlr_ready")
        left_made = sem("left_made")
        left_ready = sem("left_ready")
        hh_made = sem("hh_made")
        hh_taken = sem("hh_taken")
        xg_made = sem("xg_made")
        xg_taken = sem("xg_taken")
        score_ready = sem("score_ready")
        leaky_ready = sem("leaky_ready")
        exp1_ready = sem("exp1_ready")
        attn_ready = sem("attn_ready")
        xb_made = sem("xb_made")
        xb_taken = sem("xb_taken")
        gates_pre = sem("gates_pre")
        gates_ready = sem("gates_ready")
        xa_made = sem("xa_made")
        mix_ready = sem("mix_ready")
        sig_ready = sem("sig_ready")
        x2_ready = sem("x2_ready")
        qk_made = sem("qk_made")
        qk_taken = sem("qk_taken")
        logits_made = sem("logits_made")
        nmax_ready = sem("nmax_ready")
        exp_ready = sem("exp_ready")
        sx_made = sem("sx_made")
        sx_taken = sem("sx_taken")
        gu_made = sem("gu_made")
        gu_taken = sem("gu_taken")
        part_ready = sem("part_ready")
        part_added = sem("part_added")
        masked_ready = sem("masked_ready")
        p_turned = sem("p_turned")
        pT_ready = sem("pT_ready")
        ax_made = sem("ax_made")
        ax_taken = sem("ax_taken")
        ax_added = sem("ax_added")
        xa_turned = sem("xa_turned")
        xaT_ready = sem("xaT_ready")
        xu_made = sem("xu_made")
        xu_taken = sem("xu_taken")
        sfb_made = sem("sfb_made")
        w3_turned = sem("w3_turned")
        w3T_ready = sem("w3T_ready")
        x2_biased = sem("x2_biased")
        norm_ready = sem("norm_ready")
        x3_ready = sem("x3_ready")
        v3_made = sem("v3_made")
        v3_taken = sem("v3_taken")
        l3_made = sem("l3_made")
        l3_taken = sem("l3_taken")
        d_ready = sem("d_ready")
        dnode_ready = sem("dnode_ready")
        out_ready = sem("out_ready")
        dve_step = sem("dve_step")
        act_step = sem("act_step")
        pool_step = sem("pool_step")
        probe_ready = sem("probe_ready")
        share_ready = sem("share_ready")
        keep_step = [sem(f"keep_step{s}") for s in range(2)]
        verify_step = [sem(f"verify_step{s}") for s in range(STEPS)]
        more_step = [sem(f"more_step{s}") for s in range(STEPS)]
        full_step = [sem(f"full_step{s}") for s in range(STEPS)]

        class Chain:
            def __init__(self, eng, own):
                self.eng, self.own, self.counts, self.base = eng, own, {}, None

            def link(self, ins):
                n = self.counts[self.own] = self.counts.get(self.own, 0) + 1
                ins.then_inc(self.own, 1)
                self.eng.wait_ge(self.own, n if self.base is None else self.base + n)

            def tell(self, ins, other):
                n = self.counts[other] = self.counts.get(other, 0) + 1
                ins.then_inc(other, 1)
                self.eng.wait_ge(other, n)

        adj_rows = [adj[t * P:t * P + rows(t), :] for t in range(NT)]

        def row_tiles(dram):
            full = (NT - 1) * P
            return (dram[0:full, :].rearrange("(t p) d -> p t d", p=P), dram[full:N, :])

        def chunks(w):
            return w.rearrange("(c p) n -> p c n", p=P)

        def bcast(v):
            return v.partition_broadcast(P)

        block = ctx.enter_context(nc.Block())

        @block.sync
        def _(sp):
            xm, xt = row_tiles(x)
            sp.dma_start(xres[:, 0:NT - 1, :], xm).then_inc(x_in, 16)
            sp.dma_start(xres[0:TAIL, NT - 1, :], xt).then_inc(x_in, 16)
            for t in range(NT):
                sp.dma_start(probs[0:rows(t), t, :], adj_rows[t]).then_inc(adj_in[t], 16)
            sp.wait_ge(v_taken, NT)
            for k, u in enumerate((u1, u2)):
                sp.dma_start(wb1[:, :, k * D:(k + 1) * D], chunks(u[0])).then_inc(u12_in, 16)
            sp.wait_ge(hh_made, NT)
            for k, u in enumerate((u1, u2)):
                sp.dma_start(wb2[:, :, k * D:(k + 1) * D], chunks(u[1])).then_inc(u12b_in, 16)
            for t in range(NT):
                sp.wait_ge(x2_ready, t + 1)
                sp.dma_start(x2_dram[t * P:t * P + rows(t), :], xres[0:rows(t), t, :]).then_inc(x2_out, 16)
            sp.wait_ge(gu_made, 2 * NT)
            for s in range(STEPS):
                sp.dma_start(wb1[:, :, s * D:(s + 1) * D], chunks(u3[s])).then_inc(u3_in, 16)
            sp.dma_start(wl3, chunks(w_l3)).then_inc(w3_in, 16)
            sp.wait_ge(x2_ready, NT)
            for k, v in enumerate((gamma, beta, b_l3)):
                sp.dma_start(rowv[:, k, :], bcast(v)).then_inc(vec_in, 16)
            sp.wait_ge(sfb_made, NT)
            sp.wait_ge(x2_out, 16 * NT)
            xm, xt = row_tiles(x2_dram)
            sp.dma_start(x3[:, 0:NT - 1, :], xm).then_inc(x2_in, 16)
            sp.dma_start(x3[0:TAIL, NT - 1, :], xt).then_inc(x2_in, 16)
            for t in range(NT):
                sp.wait_ge(out_ready, t + 1)
                sp.dma_start(out[t * P:t * P + rows(t), :], xres[0:rows(t), t, :]).then_inc(y_out, 16)
            sp.wait_ge(y_out, 16 * NT)

        @block.gpsimd
        def _(pool):
            ch = Chain(pool, pool_step)
            ch.link(nc.gpsimd.memset(ident[:], 0.0))
            ch.tell(nc.gpsimd.affine_select(out=ident[:], in_=ident[:], compare_op=ALU.not_equal, fill=1.0,
                                            base=0, pattern=[[-1, P]], channel_multiplier=1), ident_ready)
            ch.tell(nc.gpsimd.memset(v0[:, :, D:D + 1], 1.0), ones_set)
            ch.tell(nc.gpsimd.memset(hh1[:, :, D:D + 1], 1.0), ones_set)
            pool.wait_ge(l0_in, 16 * 3)
            pool.wait_ge(h_ready, NT)
            for t in range(NT):
                r = rows(t)
                ch.tell(nc.gpsimd.tensor_tensor(xres[0:r, t, :], xres[0:r, t, :], rowv[0:r, 0, :], ALU.add),
                        bias_added)

            def add_part(n, t):
                r = rows(t)
                pool.wait_ge(part_ready, n + 1)
                ch.tell(nc.gpsimd.tensor_tensor(y[0:r, t, :], y[0:r, t, :], part[0:r, n % 2, :], ALU.add),
                        part_added)

            n = 0
            for t in range(NT):
                r = rows(t)
                add_part(n, t)
                n += 1
                ch.link(nc.gpsimd.tensor_tensor(y[0:r, t, :], y[0:r, t, :], h[0:r, t, :], ALU.add))
            for t in range(NT):
                add_part(n, t)
                n += 1
            for t in range(NT):
                for _ in range(2):
                    add_part(n, t)
                    n += 1
            pool.wait_ge(x2_in, 32)
            pool.wait_ge(vec_in, 48)
            for t in range(NT):
                r = rows(t)
                ch.tell(nc.gpsimd.tensor_tensor(x3[0:r, t, :], x3[0:r, t, :], rowv[0:r, 1, :], ALU.add),
                        x2_biased)

        @block.tensor
        def _(pe):
            def bank(b, r, n, at=0):
                return ps[0:r, b, at:at + n]

            def product(dst, pairs):
                for k, (lhsT, rhs) in enumerate(pairs):
                    last = pe.matmul(dst, lhsT, rhs, start=(k == 0), stop=(k == len(pairs) - 1))
                return last

            def turn_rows(k):
                for g, group in enumerate(GROUPS):
                    pe.wait_ge(h_ready, NT * k + group[-1] + 1)
                    for c in range(C):
                        for q, t in enumerate(group):
                            r = rows(t)
                            last = pe.transpose(bank(g * C + c, P, r, q * P), h[0:r, t, c * P:(c + 1) * P],
                                                ident[0:r, 0:r])
                        last.then_inc(rows_turned, 1)

            def adj_pairs(it, rhs, lhs=adjT, n=None):
                r = rows(it)
                return [(lhs[0:rows(jt), jt, it * P:it * P + r], rhs[0:rows(jt), jt, 0:n]) for jt in range(NT)]

            pe.wait_ge(ident_ready, 1)
            turn_rows(0)
            pe.wait_ge(wd_ready, 1)
            pe.wait_ge(hT_ready, 6)
            for t in range(NT):
                r, b = rows(t), 2 * (t % 3)
                hs = [hT[:, c, t * P:t * P + r] for c in range(C)]
                if t >= 3:
                    pe.wait_ge(hw_taken, t - 2)
                product(bank(b, r, D), [(hs[c], wb1[:, c, 0:D]) for c in range(C)]).then_inc(hw_made, 1)
                if t >= 3:
                    pe.wait_ge(v_taken, t - 2)
                product(bank(b + 1, r, D), [(hs[c], wb1[:, c, D:2 * D]) for c in range(C)]).then_inc(v_made, 1)
            ring = [6, 7, 0, 1, 2, 3, 4, 5]
            n = 0
            for group in GROUPS:
                for jt in range(NT):
                    if jt == 0:
                        for t in group:
                            pe.wait_ge(adj_in[t], 16)
                    if n == 2:
                        pe.wait_ge(hw_taken, NT)
                        pe.wait_ge(v_taken, NT)
                    if n >= 8:
                        pe.wait_ge(adjT_ready, n - 7)
                    for q, t in enumerate(group):
                        r = rows(t)
                        last = pe.transpose(bank(ring[n % 8], rows(jt), r, q * P),
                                            probs[0:r, t, jt * P:jt * P + rows(jt)], ident[0:r, 0:r])
                    last.then_inc(adj_turned, 1)
                    n += 1
            pe.wait_ge(adjT_ready, n)
            pe.wait_ge(l1_in, 16 * 11)
            for e in range(C):
                for c in range(C):
                    last = pe.transpose(bank(6, P, P, e * D + c * P), wb2[:, c, e * P:(e + 1) * P], ident[:])
            last.then_inc(wsa_turned, 1)
            pe.wait_ge(wsaT_ready, 1)
            for c in range(C):
                last = product(bank(7, P, 2, 2 * c),
                               [(wsaT[:, e, c * P:(c + 1) * P], cols[:, 2 * e:2 * e + 2]) for e in range(C)])
            last.then_inc(wlr_made, 1)
            pe.wait_ge(v_taken, NT)
            pe.wait_ge(hw_taken, NT)
            pe.wait_ge(wlr_ready, 1)
            pe.wait_ge(ones_set, 2)
            for it in range(NT):
                if it >= 8:
                    pe.wait_ge(l0_taken, it - 7)
                product(bank(it % 8, rows(it), D + 1), adj_pairs(it, v0, n=D + 1)).then_inc(l0_made, 1)

            pe.wait_ge(l0_taken, NT)
            turn_rows(1)
            pe.wait_ge(hT_ready, 12)
            for k, (s, w) in enumerate(SLICES):
                last = product(bank(5 + k, P, w), [(w_left[:, c, :], hT[:, c, s:s + w]) for c in range(C)])
            last.then_inc(left_made, 1)
            for t in range(NT):
                r, b = rows(t), 2 * (t % 2)
                hs = [hT[:, c, t * P:t * P + r] for c in range(C)]
                if t >= 2:
                    pe.wait_ge(xg_taken, t - 1)
                product(bank(b + 1, r, D + 5), [(hs[c], wb2[:, c, D:2 * D + 5]) for c in range(C)]).then_inc(xg_made, 1)
                if t >= 2:
                    pe.wait_ge(hh_taken, t - 1)
                product(bank(b, r, D), [(hs[c], wb2[:, c, 0:D]) for c in range(C)]).then_inc(hh_made, 1)
            pe.wait_ge(xg_taken, NT)
            pe.wait_ge(hh_taken, NT)
            pe.wait_ge(left_ready, 1)
            for it in range(NT):
                if it >= 8:
                    pe.wait_ge(xb_taken, it - 7)
                product(bank(it % 8, rows(it), D + 2), adj_pairs(it, v0, n=D + 2)).then_inc(xb_made, 1)
            pe.wait_ge(xb_taken, NT)
            pe.wait_ge(attn_ready, NT)
            for it in range(NT):
                if it >= 8:
                    pe.wait_ge(mix_ready, it - 7)
                product(bank(it % 8, rows(it), D + 1), adj_pairs(it, hh1, lhs=probs, n=D + 1)).then_inc(xa_made, 1)

            def logits(step):
                def project(w, src, b0):
                    for k, (s, n) in enumerate(SLICES):
                        product(bank(b0 + k, A, n),
                                [(w[:, c, :], src[:, c, s:s + n]) for c in range(C)]).then_inc(qk_made, 1)
                project(w13[:, :, 0:A], hT, 0)
                project(w13[:, :, A:2 * A], hT, 3)
                pe.wait_ge(qk_taken, 9 * step + 3)
                for k, (s, n) in enumerate(SLICES):
                    product(bank(k, A, n), [(w2s[:], qT[:, s:s + n])]).then_inc(qk_made, 1)
                pe.wait_ge(qk_taken, 9 * step + 9)
                for it in range(NT):
                    if it >= 2:
                        pe.wait_ge(exp_ready, NT * step + it - 1)
                    for k, (s, n) in enumerate(SLICES):
                        last = product(bank(4 * (it % 2) + k, rows(it), n),
                                       [(qwT[:, it * P:it * P + rows(it)], kT[:, s:s + n])])
                    last.then_inc(logits_made, 1)
                pe.wait_ge(exp_ready, NT * (step + 1))

            def weights_times(step):
                for t in range(NT):
                    r = rows(t)
                    m = step * NT + t
                    pe.wait_ge(masked_ready, m + 1)
                    for g, group in enumerate(GROUPS):
                        job = 3 * m + g
                        if job >= 6:
                            pe.wait_ge(pT_ready, job - 5)
                        for q, jt in enumerate(group):
                            last = pe.transpose(bank(job % 6, rows(jt), r, q * P),
                                                probs[0:r, t, jt * P:jt * P + rows(jt)], ident[0:r, 0:r])
                        last.then_inc(p_turned, 1)
                    pe.wait_ge(pT_ready, 3 * m + 3)
                    if m > NT:
                        pe.wait_ge(ax_added, t)
                    elif m >= 1:
                        pe.wait_ge(ax_taken, m)
                    product(bank(6, r, D), [(pT[0:rows(jt), m % 2, jt, 0:r], h[0:rows(jt), jt, :])
                                            for jt in range(NT)]).then_inc(ax_made, 1)
                    if step == 0:
                        pe.wait_ge(ax_taken, m + 1)
                        if t >= 1:
                            pe.wait_ge(xaT_ready, t)
                        for c in range(C):
                            last = pe.transpose(bank(7, P, r, c * P), xa_row[0:r, t % 2, c * P:(c + 1) * P],
                                                ident[0:r, 0:r])
                        last.then_inc(xa_turned, 1)

            pe.wait_ge(mix_ready, NT)
            pe.wait_ge(l2_in, 16 * 3)
            turn_rows(2)
            pe.wait_ge(hT_ready, 18)
            logits(0)
            for jt in range(NT):
                r = rows(jt)
                for c in range(C):
                    xs = h[0:r, jt, c * P:(c + 1) * P]
                    for k, (s, n) in enumerate(SLICES):
                        pe.matmul(bank(3 * c + k, P, n), xs, adjT[0:r, jt, s:s + n], start=(jt == 0), stop=False)
            for c in range(C):
                for k, (s, n) in enumerate(SLICES):
                    pe.matmul(bank(3 * c + k, P, n), ident[:], hT[:, c, s:s + n],
                              start=False, stop=True).then_inc(sx_made, 1)
            pe.wait_ge(u12_in, 32)
            pe.wait_ge(u12b_in, 32)
            pe.wait_ge(sx_taken, 2 * len(SLICES))
            for t in range(NT):
                r = rows(t)
                for k, w in enumerate((wb1, wb2)):
                    job = 2 * t + k
                    if t >= 2:
                        pe.wait_ge((part_ready, gu_taken)[k], t - 1)
                    product(bank(job % 4, r, 2 * D),
                            [(sxT[:, c, t * P:t * P + r], w[:, c, 0:2 * D]) for c in range(C)]).then_inc(gu_made, 1)
            pe.wait_ge(gu_taken, NT)
            weights_times(0)
            pe.wait_ge(xaT_ready, NT)
            logits(1)
            pe.wait_ge(u3_in, 32)
            for t in range(NT):
                r = rows(t)
                if t >= 4:
                    pe.wait_ge(xu_taken, t - 3)
                product(bank(t % 4, r, 2 * D),
                        [(hT[:, c, t * P:t * P + r], wb1[:, c, :]) for c in range(C)]).then_inc(xu_made, 1)
            pe.wait_ge(w3_in, 16)
            for e in range(C):
                for c in range(C):
                    last = pe.transpose(bank(4, P, P, c * D + e * P), wl3[:, e, c * P:(c + 1) * P], ident[:])
            last.then_inc(w3_turned, 1)
            pe.wait_ge(xu_taken, NT)
            pe.wait_ge(w3T_ready, 1)
            for it in range(NT):
                r = rows(it)
                if it >= 4:
                    pe.wait_ge(part_ready, 2 * NT + 2 * (it - 3))
                product(bank(it % 4, r, 2 * D), adj_pairs(it, fb, n=2 * D) +
                        [(ident[0:r, 0:r], fb[0:r, it, :])]).then_inc(sfb_made, 1)
            pe.wait_ge(part_ready, 4 * NT)
            weights_times(1)

            pe.wait_ge(ax_added, NT)
            turn_rows(3)
            pe.wait_ge(hT_ready, 24)
            for t in range(NT):
                r = rows(t)
                if t >= 8:
                    pe.wait_ge(v3_taken, t - 7)
                product(bank(t % 8, r, D), [(hT[:, c, t * P:t * P + r], wb1[:, c, 0:D]) for c in range(C)]
                        ).then_inc(v3_made, 1)
            pe.wait_ge(v3_taken, NT)
            for it in range(NT):
                r = rows(it)
                if it >= 8:
                    pe.wait_ge(l3_taken, it - 7)
                product(bank(it % 8, r, D), adj_pairs(it, y, n=D) + [(ident[0:r, 0:r], y[0:r, it, :])]
                        ).then_inc(l3_made, 1)

        @block.scalar
        def _(act):
            ch = Chain(act, act_step)
            act.dma_start(wb1[:, :, 0:D], chunks(w0)).then_inc(l0_in, 16)
            act.dma_start(cols[:, 6:6 + C], diag1.rearrange("(c p) -> p c", p=P)).then_inc(l0_in, 16)
            act.dma_start(rowv[:, 0, :], bcast(bias0)).then_inc(l0_in, 16)
            act.dma_start(wb2[:, :, 0:D], chunks(w_sa)).then_inc(l1_in, 16)
            act.dma_start(wb2[:, :, D:2 * D], chunks(w_gcnb)).then_inc(l1_in, 16)
            for k, w in enumerate((wa, wb)):
                for s in range(2):
                    act.dma_start(wb2[:, :, 2 * D + k + 2 * s],
                                  w[0, s * D:(s + 1) * D].rearrange("(c p) -> p c", p=P)).then_inc(l1_in, 16)
            for s in range(2):
                act.dma_start(cols[:, s:2 * C:2],
                              a_sa[0, s * D:(s + 1) * D].rearrange("(c p) -> p c", p=P)).then_inc(l1_in, 16)
            act.dma_start(rowv[:, 1, :], bcast(b_gcnb)).then_inc(l1_in, 16)
            act.dma_start(cols[:, 8:9], bcast(ba)).then_inc(l1_in, 16)
            act.dma_start(cols[:, 9:10], bcast(bb)).then_inc(l1_in, 16)
            act.dma_start(w13[:, :, 0:A], chunks(w1)).then_inc(l2_in, 16)
            act.dma_start(w13[:, :, A:2 * A], chunks(w3)).then_inc(l2_in, 16)
            act.dma_start(w2s[:], w2).then_inc(l2_in, 16)

            def norm_rows(k, g, dst, src, func, done):
                n, group = len(GROUPS) * k + g, GROUPS[g]
                some = slice(group[0], group[-1] + 1)
                act.wait_ge(scale_ready, n + 1)
                ch.tell(nc.scalar.activation(S["std"][:, some], S["var"][:, some], ACT.Sqrt, bias=cols[:, 10:11]),
                        std_ready)
                act.wait_ge(rstd_ready, n + 1)
                for t in group:
                    r = rows(t)
                    ch.tell(nc.scalar.activation(dst[0:r, t, :], src[0:r, t, :], func,
                                                 bias=S["shift"][0:r, t:t + 1], scale=S["rstd"][0:r, t:t + 1]), done)

            for g in range(len(GROUPS)):
                norm_rows(0, g, h, xres, ACT.Relu, h_ready)
            act.wait_ge(ones_set, 1)
            for t in range(NT):
                r = rows(t)
                act.wait_ge(v_made, t + 1)
                ch.tell(nc.scalar.copy(v0[0:r, t, 0:D], ps[0:r, 2 * (t % 3) + 1, 0:D]), v_taken)
            ring = [6, 7, 0, 1, 2, 3, 4, 5]
            n = 0
            for g, group in enumerate(GROUPS):
                w = width(group)
                for jt in range(NT):
                    r = rows(jt)
                    act.wait_ge(adj_turned, n + 1)
                    ch.tell(nc.scalar.activation(adjT[0:r, jt, g * BANK:g * BANK + w], ps[0:r, ring[n % 8], 0:w],
                                                 ACT.Copy, accum_out=S[f"col{g}"][0:r, jt:jt + 1]), adjT_ready)
                    n += 1
            for g in range(len(GROUPS)):
                norm_rows(1, g, h, xres, ACT.Relu, h_ready)
            act.wait_ge(left_made, 1)
            for k, (s, w) in enumerate(SLICES):
                ins = nc.scalar.copy(left[:, s:s + w], ps[:, 5 + k, 0:w])
                if k < len(SLICES) - 1:
                    ch.link(ins)
                else:
                    ch.tell(ins, left_ready)
            for t in range(NT):
                r = rows(t)
                act.wait_ge(hh_made, t + 1)
                ch.tell(nc.scalar.copy(hh1[0:r, t, 0:D], ps[0:r, 2 * (t % 2), 0:D]), hh_taken)
            act.wait_ge(xg_taken, NT)
            for t in range(NT):
                r = rows(t)
                ch.tell(nc.scalar.activation(probs[0:r, t, :], left[0:r, :], ACT.Identity,
                                             bias=gpre[0:r, t, 2:3]), score_ready)
            for t in range(NT):
                r = rows(t)
                act.wait_ge(leaky_ready, t + 1)
                ch.tell(nc.scalar.activation(probs[0:r, t, :], probs[0:r, t, :], ACT.Exp, scale=-1.0), exp1_ready)
            act.wait_ge(gates_pre, 1)
            ch.tell(nc.scalar.activation(gates[:], gates[:], ACT.Sigmoid), gates_ready)
            for g, group in enumerate(GROUPS):
                for t in group:
                    r = rows(t)
                    act.wait_ge(mix_ready, t + 1)
                    ch.tell(nc.scalar.activation(y[0:r, t, :], y[0:r, t, :], ACT.Sigmoid), sig_ready)
                norm_rows(2, g, h, xres, ACT.Relu, h_ready)

            def softmax_rows(step):
                for t in range(NT):
                    r = rows(t)
                    b = 4 * (t % 2) * BANK
                    act.wait_ge(nmax_ready, NT * step + t + 1)
                    ch.tell(nc.scalar.activation(probs[0:r, t, :], psf[0:r, b:b + N], ACT.Exp,
                                                 bias=S["nmax"][0:r, t:t + 1],
                                                 accum_out=S["zsum"][0:r, t:t + 1]), exp_ready)

            def share_mass(n):
                act.wait_ge(probe_ready, n + 1)
                for t in range(NT - SHARED, NT):
                    r = rows(t)
                    limit = S["spred"][0:r, t:t + 1]
                    ch.link(nc.scalar.activation(waste[0:r, :], probs[0:r, t, :], ACT.Relu, bias=limit,
                                                 accum_out=S["ssum"][0:r, t:t + 1]))
                    ins = nc.scalar.activation(waste[0:r, :], waste[0:r, :], ACT.Sign,
                                               accum_out=S["scount"][0:r, t:t + 1])
                    if t < NT - 1:
                        ch.link(ins)
                    else:
                        ch.tell(ins, share_ready)

            parts = [0]

            def part_out(src, scale, r):
                n = parts[0]
                if n >= 2:
                    act.wait_ge(part_added, n - 1)
                ins = nc.scalar.activation(part[0:r, n % 2, :], src, ACT.Copy, scale=scale)
                parts[0] += 1
                return ins

            def turned_weights(step, t):
                r = rows(t)
                m = step * NT + t
                for g, group in enumerate(GROUPS):
                    job = 3 * m + g
                    act.wait_ge(p_turned, job + 1)
                    if m >= 2 and g == 0:
                        act.wait_ge(ax_made, m - 1)
                    full = [jt for jt in group if rows(jt) == P]
                    k = len(full)
                    src = ps[:, job % 6, 0:k * P].rearrange("p (q n) -> p q n", n=P)[:, :, 0:r]
                    ins = nc.scalar.copy(pT[:, m % 2, group[0]:group[0] + k, 0:r], src)
                    if k == len(group):
                        ch.tell(ins, pT_ready)
                    else:
                        ch.link(ins)
                        jt = group[-1]
                        ch.tell(nc.scalar.copy(pT[0:rows(jt), m % 2, jt, 0:r],
                                               ps[0:rows(jt), job % 6, k * P:k * P + r]), pT_ready)

            softmax_rows(0)
            for k in range(1 + 2 * PAIRS[0]):
                share_mass(k)
            for c in range(C):
                for k, (s, n) in enumerate(SLICES):
                    act.wait_ge(sx_made, 3 * c + k + 1)
                    ch.tell(nc.scalar.copy(sxT[:, c, s:s + n], ps[:, 3 * c + k, 0:n]), sx_taken)
            for t in range(NT):
                r = rows(t)
                dr, dc = S["rinv"][0:r, t:t + 1], S["cinv"][0:r, t:t + 1]
                act.wait_ge(gu_made, 2 * t + 1)
                b = (2 * t) % 4
                ch.link(nc.scalar.activation(y[0:r, t, :], ps[0:r, b, 0:D], ACT.Copy, scale=dr))
                ch.tell(part_out(ps[0:r, b, D:2 * D], dc, r), part_ready)
                act.wait_ge(gu_made, 2 * t + 2)
                ch.link(nc.scalar.activation(fb[0:r, t, 0:D], ps[0:r, b + 1, 0:D], ACT.Copy, scale=dr))
                ch.tell(nc.scalar.activation(fb[0:r, t, D:2 * D], ps[0:r, b + 1, D:2 * D], ACT.Copy, scale=dc),
                        gu_taken)
            for t in range(NT):
                r = rows(t)
                turned_weights(0, t)
                act.wait_ge(ax_made, t + 1)
                if t >= 2:
                    act.wait_ge(xa_turned, t - 1)
                ch.tell(nc.scalar.activation(xa_row[0:r, t % 2, :], ps[0:r, 6, 0:D], ACT.Copy,
                                             scale=S["kinv"][0:r, t:t + 1]), ax_taken)
                act.wait_ge(xa_turned, t + 1)
                ch.tell(nc.scalar.copy(hT[:, :, t * P:t * P + r],
                                       ps[:, 7, 0:C * P].rearrange("p (c n) -> p c n", c=C)[:, :, 0:r]), xaT_ready)
            softmax_rows(1)
            probes = 1 + 2 * PAIRS[1]
            xu_probes, sfb_from = 2, 3

            def spread(k, first, last):
                if not first <= k <= last:
                    return range(0)
                n = last - first + 1
                return range(NT * (k - first) // n, NT * (k - first + 1) // n)

            for k in range(probes):
                share_mass(1 + 2 * PAIRS[0] + k)
                for t in spread(k, 0, xu_probes - 1):
                    r = rows(t)
                    act.wait_ge(xu_made, t + 1)
                    ch.tell(part_out(ps[0:r, t % 4, 0:D], 1.0, r), part_ready)
                    ch.tell(nc.scalar.copy(h[0:r, t, :], ps[0:r, t % 4, D:2 * D]), xu_taken)
                if k == xu_probes:
                    act.wait_ge(w3_turned, 1)
                    ch.tell(nc.scalar.copy(wb1[:, :, 0:D], ps[:, 4, :].rearrange("p (c n) -> p c n", c=C)),
                            w3T_ready)
                for t in spread(k, sfb_from, probes - 1):
                    r = rows(t)
                    dr, dc = S["rinv"][0:r, t:t + 1], S["cinv"][0:r, t:t + 1]
                    act.wait_ge(sfb_made, t + 1)
                    ch.tell(part_out(ps[0:r, t % 4, 0:D], dr, r), part_ready)
                    ch.tell(part_out(ps[0:r, t % 4, D:2 * D], dc, r), part_ready)
            for t in range(NT + 1):
                if t < NT:
                    turned_weights(1, t)
                for g, group in enumerate(GROUPS):
                    if t == group[-1] + 1:
                        norm_rows(3, g, y, y, ACT.Identity, norm_ready)
            act.wait_ge(d_ready, 1)
            ch.tell(nc.scalar.activation(S["dnode"], S["dinv"], ACT.Sqrt), dnode_ready)
            for g in range(len(GROUPS)):
                norm_rows(4, g, h, x3, ACT.Relu, h_ready)

        @block.vector
        def _(dve):
            ch = Chain(dve, dve_step)
            V = nc.vector
            ch.link(V.memset(stat[:], 1.0))
            ch.link(V.memset(top8[:], 1.0))
            ch.link(V.memset(gates[:], 0.0))
            ch.link(V.memset(gpre[:], 0.0))
            ch.link(V.memset(cols[:, 10:11], LN_EPS))
            ch.link(V.memset(sq32[:], 0.0))

            def stats_of(src, t):
                r = rows(t)
                ch.link(V.bn_stats(bn6[0:r, :], src))
                aggr = V.bn_aggr(stat[0:r, 0:2, t], bn6[0:r, :])
                group = next(g for g in GROUPS if t in g)
                if t < group[-1]:
                    ch.link(aggr)
                    return
                ch.tell(aggr, scale_ready)
                some = slice(group[0], t + 1)
                dve.wait_ge(std_ready, ch.counts[scale_ready])
                ch.link(V.reciprocal(S["rstd"][:, some], S["std"][:, some]))
                ch.tell(V.scalar_tensor_tensor(S["shift"][:, some], S["mean"][:, some], -1.0, S["rstd"][:, some],
                                               ALU.mult, ALU.mult), rstd_ready)

            def take_turned(k):
                for g, group in enumerate(GROUPS):
                    w = width(group)
                    for c in range(C):
                        dve.wait_ge(rows_turned, 6 * k + g * C + c + 1)
                        ch.tell(V.tensor_copy(hT[:, c, g * BANK:g * BANK + w], ps[:, g * C + c, 0:w]), hT_ready)

            dve.wait_ge(x_in, 32)
            for t in range(NT):
                stats_of(xres[0:rows(t), t, :], t)
            dve.wait_ge(l0_in, 16 * 3)
            ch.link(V.tensor_scalar(cols[:, 6:6 + C], cols[:, 6:6 + C], 1.0, None, ALU.add))
            for c in range(C):
                ins = V.tensor_scalar(wb1[:, c, D:2 * D], wb1[:, c, 0:D], cols[:, 6 + c:7 + c], None, ALU.mult)
                if c < C - 1:
                    ch.link(ins)
                else:
                    ch.tell(ins, wd_ready)
            take_turned(0)
            for t in range(NT):
                r = rows(t)
                dve.wait_ge(hw_made, t + 1)
                dve.wait_ge(bias_added, t + 1)
                ch.tell(V.tensor_tensor(xres[0:r, t, :], xres[0:r, t, :], ps[0:r, 2 * (t % 3), 0:D], ALU.add),
                        hw_taken)
            dve.wait_ge(wsa_turned, 1)
            ch.tell(V.tensor_copy(wsaT, ps[:, 6, :].rearrange("p (c n) -> p c n", c=C)), wsaT_ready)
            dve.wait_ge(wlr_made, 1)
            for c in range(C):
                ch.link(V.memset(w_left[:, c, :], 1.0))
                ch.link(V.tensor_scalar(w_left[:, c, :], w_left[:, c, :], ps[:, 7, 2 * c:2 * c + 1], None, ALU.mult))
                ins = V.tensor_copy(wb2[:, c, 2 * D + 4:2 * D + 5], ps[:, 7, 2 * c + 1:2 * c + 2])
                if c < C - 1:
                    ch.link(ins)
                else:
                    ch.tell(ins, wlr_ready)
            for t in range(NT):
                r = rows(t)
                dve.wait_ge(l0_made, t + 1)
                ch.link(V.tensor_tensor(xres[0:r, t, :], xres[0:r, t, :], ps[0:r, t % 8, 0:D], ALU.subtract))
                ch.tell(V.tensor_copy(S["rowsum"][0:r, t:t + 1], ps[0:r, t % 8, D:D + 1]), l0_taken)
                stats_of(xres[0:r, t, :], t)
            ch.link(V.tensor_scalar(S["rinv"], S["rowsum"], 1.0, 1e-12, ALU.add, ALU.max))
            ch.link(V.reciprocal(S["rinv"], S["rinv"]))
            ch.link(V.tensor_tensor(S["cinv"], S["col0"], S["col1"], ALU.add))
            ch.link(V.tensor_tensor(S["cinv"], S["cinv"], S["col2"], ALU.add))
            ch.link(V.tensor_scalar(S["cinv"], S["cinv"], 1.0, 1e-12, ALU.add, ALU.max))
            ch.link(V.reciprocal(S["cinv"], S["cinv"]))
            ch.link(V.tensor_scalar(S["dinv"], S["rowsum"], 1.0, None, ALU.add))
            ch.tell(V.reciprocal(S["dinv"], S["dinv"]), d_ready)
            take_turned(1)
            dve.wait_ge(l1_in, 16 * 11)
            for t in range(NT):
                r = rows(t)
                dve.wait_ge(xg_made, t + 1)
                b = 2 * (t % 2) + 1
                ch.link(V.tensor_copy(v0[0:r, t, :], ps[0:r, b, 0:D + 2]))
                ch.tell(V.tensor_copy(gpre[0:r, t, :], ps[0:r, b, D + 2:D + 5]), xg_taken)
            for t in range(NT):
                row = probs[0:rows(t), t, :]
                dve.wait_ge(score_ready, t + 1)
                ch.tell(V.scalar_tensor_tensor(row, row, SLOPE, row, ALU.mult, ALU.max), leaky_ready)
            for t in range(NT):
                r = rows(t)
                dve.wait_ge(exp1_ready, t + 1)
                ch.tell(V.scalar_tensor_tensor(probs[0:r, t, :], adjT[0:r, t, :], 0.0, probs[0:r, t, :],
                                               ALU.not_equal, ALU.mult), attn_ready)
            for t in range(NT):
                r = rows(t)
                dve.wait_ge(xb_made, t + 1)
                ch.link(V.tensor_tensor(y[0:r, t, :], ps[0:r, t % 8, 0:D], rowv[0:r, 1, :], ALU.add))
                ch.tell(V.tensor_tensor(gates[0:r, t, :], ps[0:r, t % 8, D:D + 2], gpre[0:r, t, 0:2], ALU.add),
                        xb_taken)
            ch.link(V.tensor_scalar(gates[:, :, 0], gates[:, :, 0], cols[:, 8:9], None, ALU.add))
            ch.tell(V.tensor_scalar(gates[:, :, 1], gates[:, :, 1], cols[:, 9:10], None, ALU.add), gates_pre)
            dve.wait_ge(gates_ready, 1)

            def mix(t):
                r = rows(t)
                dve.wait_ge(xa_made, t + 1)
                ratio = S["f1"][0:r, t:t + 1]
                ch.link(V.tensor_scalar(ratio, ps[0:r, t % 8, D:D + 1], SOFT_EPS, None, ALU.add))
                ch.link(V.reciprocal(ratio, ratio))
                ch.link(V.tensor_tensor(ratio, ratio, gates[0:r, t, 0:1], ALU.mult))
                ch.link(V.tensor_scalar(y[0:r, t, :], y[0:r, t, :], gates[0:r, t, 1:2], None, ALU.mult))
                ch.tell(V.scalar_tensor_tensor(y[0:r, t, :], ps[0:r, t % 8, 0:D], ratio, y[0:r, t, :],
                                               ALU.mult, ALU.add), mix_ready)

            def residual(t):
                r = rows(t)
                dve.wait_ge(sig_ready, t + 1)
                ch.tell(V.tensor_tensor(xres[0:r, t, :], xres[0:r, t, :], y[0:r, t, :], ALU.add), x2_ready)
                stats_of(xres[0:r, t, :], t)

            for t in range(NT + 1):
                if t < NT:
                    mix(t)
                if t >= 1:
                    residual(t - 1)
            take_turned(2)
            dve.wait_ge(x2_out, 16 * NT)

            def project_out(step):
                for k in range(9):
                    s, n = SLICES[k % 3]
                    dst = (qT, kT, qwT)[k // 3]
                    b = k if k < 6 else k - 6
                    dve.wait_ge(qk_made, 9 * step + k + 1)
                    ch.tell(V.tensor_copy(dst[:, s:s + n], ps[0:A, b, 0:n]), qk_taken)

            def maxima(step):
                for t in range(NT):
                    r = rows(t)
                    b = 4 * (t % 2) * BANK
                    dve.wait_ge(logits_made, NT * step + t + 1)
                    ch.tell(V.tensor_reduce(S["nmax"][0:r, t:t + 1], psf[0:r, b:b + N], AX_X, ALU.max, negate=True),
                            nmax_ready)

            def mass_above(c, limit, mass):
                for t in range(NT):
                    r = rows(t)
                    c.link(V.scalar_tensor_tensor(masked[0:r, :], probs[0:r, t, :], limit[0:r, t:t + 1],
                                                  probs[0:r, t, :], ALU.is_ge, ALU.mult,
                                                  accum_out=mass[0:r, t:t + 1]))

            def mass_shared(c, n):
                theirs = slice(NT - SHARED, NT)
                V.tensor_scalar(S["spred"][:, theirs], S["probe"][:, theirs], -BELOW, None, ALU.mult).then_inc(
                    probe_ready, 1)
                dve.wait_ge(probe_ready, n + 1)
                for t in range(NT - SHARED):
                    c.link(V.scalar_tensor_tensor(masked, probs[:, t, :], S["probe"][:, t:t + 1], probs[:, t, :],
                                                  ALU.is_ge, ALU.mult, accum_out=S["mass"][:, t:t + 1]))
                dve.wait_ge(share_ready, n + 1)
                c.link(V.tensor_tensor(S["scount"][:, theirs], S["scount"][:, theirs], S["spred"][:, theirs],
                                       ALU.mult))
                c.link(V.tensor_tensor(S["mass"][:, theirs], S["ssum"][:, theirs], S["scount"][:, theirs],
                                       ALU.subtract))

            def narrow(c, shared=None):
                if shared is None:
                    mass_above(c, S["probe"], S["mass"])
                else:
                    mass_shared(c, shared)
                c.link(V.tensor_tensor(S["reached"], S["mass"], S["goal"], ALU.is_ge))
                c.link(V.tensor_tensor(S["missed"], S["mass"], S["goal"], ALU.is_lt))
                c.link(V.tensor_tensor(chosen, probe_mass, verdicts, ALU.mult))
                c.link(V.tensor_tensor(lo_mhi, lo_mhi, chosen, ALU.max))
                c.link(V.scalar_tensor_tensor(chosen, verdicts, HUGE, probe_mass, ALU.mult, ALU.max))
                c.link(V.tensor_tensor(hi_mlo, hi_mlo, chosen, ALU.min))

            def midpoint(c):
                c.link(V.tensor_tensor(S["w1"], S["hi"], S["lo"], ALU.subtract))
                c.link(V.scalar_tensor_tensor(S["probe"], S["w1"], 0.5, S["lo"], ALU.mult, ALU.add))

            def interpolate(c):
                c.link(V.tensor_tensor(gaps, hi_mlo, lo_mhi, ALU.subtract))
                c.link(V.scalar_tensor_tensor(S["f1"], S["lo"], AHEAD, S["mlo"], ALU.mult, ALU.add))
                c.link(V.tensor_tensor(S["f1"], S["f1"], S["goal"], ALU.subtract))
                c.link(V.reciprocal(S["f2"], S["w2"]))
                c.link(V.tensor_tensor(S["f1"], S["f1"], S["f2"], ALU.mult))
                c.link(V.tensor_scalar(S["f1"], S["f1"], CLIP_LO, CLIP_HI, ALU.max, ALU.min))
                c.link(V.tensor_tensor(S["f1"], S["f1"], S["w1"], ALU.mult))
                c.link(V.tensor_tensor(S["probe"], S["lo"], S["f1"], ALU.add))

            def threshold(c):
                for t in range(NT):
                    r = rows(t)
                    c.link(V.scalar_tensor_tensor(masked[0:r, :], probs[0:r, t, :], S["hi"][0:r, t:t + 1],
                                                  probs[0:r, t, :], ALU.is_lt, ALU.mult))
                    c.link(V.max(top8[0:r, 0, t, :], masked[0:r, :]))
                vals, sums = top8[:, 0, :, :], top8[:, 1, :, :]
                c.link(V.tensor_tensor(sums[:, :, 0], vals[:, :, 0], S["mhi"], ALU.add))
                for k in range(1, 8):
                    c.link(V.tensor_tensor(sums[:, :, k], sums[:, :, k - 1], vals[:, :, k], ALU.add))
                goal8 = S["goal"].unsqueeze(2).broadcast_to([P, NT, 8])
                c.link(V.tensor_tensor(sums, sums, goal8, ALU.is_ge))
                c.link(V.tensor_scalar(S["open"], sums[:, :, 7], 0.5, None, ALU.is_lt))
                c.link(V.tensor_tensor(sums, sums, vals, ALU.mult))
                c.link(V.tensor_reduce(S["tstar"], sums, AX_X, ALU.max))
                c.link(V.tensor_tensor(S["tstar"], S["tstar"], vals[:, :, 7], ALU.max))
                t8 = S["tstar"].unsqueeze(2).broadcast_to([P, NT, 8])
                c.link(V.tensor_tensor(sums, vals, t8, ALU.is_gt))
                c.link(V.tensor_tensor(sums, sums, vals, ALU.mult))
                c.link(V.tensor_reduce(S["above"], sums, AX_X, ALU.add))
                c.link(V.tensor_tensor(S["above"], S["above"], S["mhi"], ALU.add))
                c.link(V.tensor_tensor(S["allow"], S["goal"], S["above"], ALU.subtract))
                c.link(V.reciprocal(S["f1"], S["tstar"]))
                c.link(V.tensor_tensor(S["allow"], S["allow"], S["f1"], ALU.mult))
                c.link(V.tensor_scalar(S["allow"], S["allow"], 1.0, None, ALU.add))
                c.link(V.tensor_tensor(sums, vals, t8, ALU.is_equal))
                c.link(V.tensor_reduce(S["f1"], sums, AX_X, ALU.add))
                c.link(V.scalar_tensor_tensor(S["f2"], S["f1"], 0.25, S["allow"], ALU.add, ALU.is_ge))
                c.link(V.scalar_tensor_tensor(S["f2"], S["f1"], 1.5, S["f2"], ALU.is_gt, ALU.mult))
                c.link(V.tensor_tensor(S["partial"], S["f2"], sums[:, :, 7], ALU.max))

            PROBE = NT + 6
            MORE_PAIR = 2 * PROBE + 2 + 8
            PAIR = 2 * (PROBE - SHARED + 2) + 2 + 8

            def search(step):
                ch.link(V.tensor_scalar(S["goal"], S["zsum"], P_NUC, None, ALU.mult))
                ch.link(V.tensor_scalar(S["lo"], S["zsum"], LEAST, None, ALU.mult))
                ch.link(V.tensor_copy(S["mlo"], S["zsum"]))
                ch.link(V.memset(S["hi"], 1.5))
                ch.link(V.memset(S["mhi"], 0.0))
                ch.link(V.tensor_scalar(S["probe"], S["lo"], FIRST_PROBE, 0.75, ALU.mult, ALU.min))
                first = sum(1 + 2 * n for n in PAIRS[:step])
                narrow(ch, first)
                base = ch.counts[dve_step]
                with dve.Fori(0, PAIRS[step]) as i:
                    ch.counts[dve_step] = 0
                    ch.base = i * PAIR + base
                    midpoint(ch)
                    narrow(ch, i * 2 + (first + 1))
                    interpolate(ch)
                    narrow(ch, i * 2 + (first + 2))
                    assert ch.counts[dve_step] == PAIR
                ch.base = None
                ch.counts[dve_step] = base + PAIR * PAIRS[step]
                threshold(ch)
                with dve.If(any_row(ch, S["open"]) > 0):
                    verify = Chain(dve, verify_step[step])
                    recheck(verify)
                    with dve.If(any_row(verify, S["open"]) > 0):
                        more = Chain(dve, more_step[step])
                        with dve.Fori(0, MORE_PAIRS) as i:
                            more.base = i * MORE_PAIR
                            more.counts[more_step[step]] = 0
                            midpoint(more)
                            narrow(more)
                            interpolate(more)
                            narrow(more)
                            assert more.counts[more_step[step]] == MORE_PAIR
                        more.base = None
                        more.counts[more_step[step]] = MORE_PAIRS * MORE_PAIR
                        threshold(more)
                        recheck(more)
                        with dve.If(any_row(more, S["open"]) > 0):
                            full = Chain(dve, full_step[step])
                            with dve.Fori(0, FULL_PROBES) as i:
                                full.base = i * (PROBE + 2)
                                full.counts[full_step[step]] = 0
                                midpoint(full)
                                narrow(full)
                            full.base = None
                            full.counts[full_step[step]] = FULL_PROBES * (PROBE + 2)
                            threshold(full)

            def recheck(c):
                mass_above(c, S["tstar"], S["mass"])
                c.link(V.tensor_tensor(S["missed"], S["mass"], S["goal"], ALU.is_lt))
                c.link(V.tensor_tensor(S["open"], S["open"], S["missed"], ALU.mult))

            def any_row(c, col):
                c.link(V.tensor_reduce(sq32[:, 0, 0:1], col, AX_X, ALU.max))
                c.link(V.transpose(sq32[:, 1, :], sq32[:, 0, :]))
                c.link(V.tensor_reduce(cols[:, 12:13], sq32[:, 1, :], AX_X, ALU.max))
                for q in range(4):
                    c.link(V.tensor_copy(flag[:, q:q + 1], cols[32 * q:32 * q + 1, 12:13]))
                c.link(V.tensor_reduce(flag[:, 4:5], flag[:, 0:4], AX_X, ALU.max))
                c.link(V.tensor_copy(flag_i[:, 0:1], flag[:, 4:5]))
                return dve.value_load(flag_i[0:1, 0:1], min_val=0, max_val=1)

            def keep(c, t):
                r = rows(t)
                row, ts = probs[0:r, t, :], S["tstar"][0:r, t:t + 1]
                c.link(V.scalar_tensor_tensor(masked[0:r, :], row, ts, row, ALU.is_gt, ALU.mult))
                c.link(V.tensor_scalar(tie[0:r, :], row, ts, None, ALU.is_equal))
                c.link(V.tensor_tensor_scan(order[0:r, :], tie[0:r, :], tie[0:r, :], 0.0, ALU.add, ALU.max))
                c.link(V.scalar_tensor_tensor(tie[0:r, :], order[0:r, :], S["allow"][0:r, t:t + 1], tie[0:r, :],
                                              ALU.is_lt, ALU.mult))
                c.link(V.scalar_tensor_tensor(row, tie[0:r, :], ts, masked[0:r, :], ALU.mult, ALU.add,
                                              accum_out=S["kept"][0:r, t:t + 1]))
                c.tell(V.reciprocal(S["kinv"][0:r, t:t + 1], S["kept"][0:r, t:t + 1]), masked_ready)

            def keep_whole(c, t):
                r = rows(t)
                row = probs[0:r, t, :]
                c.link(V.scalar_tensor_tensor(row, row, S["tstar"][0:r, t:t + 1], row, ALU.is_ge, ALU.mult,
                                              accum_out=S["kept"][0:r, t:t + 1]))
                c.tell(V.reciprocal(S["kinv"][0:r, t:t + 1], S["kept"][0:r, t:t + 1]), masked_ready)

            def add_attended(t):
                r = rows(t)
                dve.wait_ge(ax_made, NT + t + 1)
                row = y[0:r, t, :]
                ch.tell(V.scalar_tensor_tensor(row, ps[0:r, 6, 0:D], S["kinv"][0:r, t:t + 1], row,
                                               ALU.mult, ALU.add), ax_added)
                stats_of(row, t)

            project_out(0)
            maxima(0)
            dve.wait_ge(exp_ready, NT)
            search(0)
            with dve.If(any_row(ch, S["partial"]) > 0):
                some = Chain(dve, keep_step[0])
                for t in range(NT):
                    keep(some, t)
            with dve.Else():
                whole = Chain(dve, keep_step[1])
                for t in range(NT):
                    keep_whole(whole, t)
            ch.counts[masked_ready] = NT
            project_out(1)
            maxima(1)
            dve.wait_ge(exp_ready, 2 * NT)
            search(1)
            dve.wait_ge(part_added, 4 * NT)
            for t in range(NT + 1):
                if t < NT:
                    keep(ch, t)
                if t >= 1:
                    add_attended(t - 1)
            dve.wait_ge(vec_in, 48)
            for t in range(NT):
                r = rows(t)
                dve.wait_ge(norm_ready, t + 1)
                ch.link(V.tensor_tensor(y[0:r, t, :], y[0:r, t, :], rowv[0:r, 0, :], ALU.mult))
                dve.wait_ge(x2_biased, t + 1)
                ch.link(V.tensor_tensor(x3[0:r, t, :], x3[0:r, t, :], y[0:r, t, :], ALU.add))
                stats_of(x3[0:r, t, :], t)
            take_turned(3)
            dve.wait_ge(dnode_ready, 1)
            for t in range(NT):
                r = rows(t)
                dve.wait_ge(v3_made, t + 1)
                ch.tell(V.tensor_scalar(y[0:r, t, :], ps[0:r, t % 8, 0:D], S["dnode"][0:r, t:t + 1], None,
                                        ALU.mult), v3_taken)
            for t in range(NT):
                r = rows(t)
                dve.wait_ge(l3_made, t + 1)
                o = xres[0:r, t, :]
                ch.tell(V.scalar_tensor_tensor(o, ps[0:r, t % 8, 0:D], S["dnode"][0:r, t:t + 1], rowv[0:r, 2, :],
                                               ALU.mult, ALU.add), l3_taken)
                ch.tell(V.scalar_tensor_tensor(o, o, 0.0, x3[0:r, t, :], ALU.max, ALU.add), out_ready)


INS = ("x", "adj", "L0_gnn_weight", "L0_gnn_learnable_diag_1", "L0_gnn_bias", "L1_gnn_W_sa", "L1_gnn_a_sa",
       "L1_gnn_W_gcnb", "L1_gnn_b_gcnb", "L1_gnn_Wa", "L1_gnn_ba", "L1_gnn_Wb", "L1_gnn_bb", "L2_gnn_W1",
       "L2_gnn_W2", "L2_gnn_W3", "L2_gnn_U1", "L2_gnn_U2", "L2_gnn_U3", "L2_gnn_gamma", "L2_gnn_beta",
       "L3_gnn_W", "L3_gnn_b")


def kernel(**inputs):
    import numpy as np
    import concourse.bacc as bacc
    from concourse.bass_utils import run_bass_kernel_spmd

    nc = bacc.Bacc("TRN2", target_bir_lowering=False, num_devices=1, dynamic_dma_scratch_size=4096)
    arrays, args = {}, []
    for name in INS:
        a = np.ascontiguousarray(inputs[name])
        arrays[f"in_{name}"] = a
        args.append(nc.dram_tensor(f"in_{name}", a.shape, mybir.dt.from_np(a.dtype), kind="ExternalInput").ap())
    out = nc.dram_tensor("out_rows", inputs["x"].shape, F32, kind="ExternalOutput").ap()
    gnn_stack(nc, *args, out)
    result = run_bass_kernel_spmd(nc, [arrays], core_ids=[0])
    return result.results[0]["out_rows"]
```

```python
from contextlib import ExitStack

import numpy as np

import concourse.bass as bass
from concourse import mybir

P = 128
ALU = mybir.AluOpType
ACT = mybir.ActivationFunctionType
F32 = mybir.dt.float32
F32R = mybir.dt.float32r
BF16 = mybir.dt.bfloat16
F16 = mybir.dt.float16
I32 = mybir.dt.int32
AX_X = mybir.AxisListType.X
BANK = 512
LN_EPS = 1e-5
SOFT_EPS = 1e-5
SLOPE = 0.01
P_NUC = 0.9
STEPS = 2
PAIRS = (1, 6)
MORE_PAIRS = 2
GU_EARLY = 8
GU_PROBES = range(0, 3)
SFB_PROBES = range(3, 13)
SHARED = 4
BELOW = 1.0 - 2.0 ** -24
FULL_PROBES = 40
FIRST_PROBE = 12.0
AHEAD = 6.0
CLIP_LO, CLIP_HI = 0.04, 0.9
HUGE = 1e30


def gnn_stack(nc, x, adj, w0, diag1, bias0, w_sa, a_sa, w_gcnb, b_gcnb, wa, ba, wb, bb,
              w1, w2, w3, u1, u2, u3, gamma, beta, w_l3, b_l3, out):
    N, D = x.shape
    NT = -(-N // P)
    TAIL = N - (NT - 1) * P
    C = D // P
    A = w1.shape[1]
    GROUPS = [range(g, min(g + 4, NT)) for g in range(0, NT, 4)]
    SLICES = [(s, min(BANK, N - s)) for s in range(0, N, BANK)]
    LEAST = (1.0 - P_NUC) / N * 0.999

    def rows(t):
        return P if t < NT - 1 else TAIL

    def width(group):
        return sum(rows(t) for t in group)

    with ExitStack() as ctx:
        def sb(name, shape, dt=F32):
            return ctx.enter_context(nc.sbuf_tensor(name, shape, dt))

        def shared(name, shape, parts_name):
            with nc.sbuf_tensor(name, shape, F32) as plain:
                pass
            flat = [shape[0], int(np.prod(shape[1:]))]
            return plain, sb(parts_name, flat, F32R)

        def sem(name):
            return ctx.enter_context(nc.semaphore(name))

        ctx.enter_context(nc.allow_non_contiguous_dma(reason="weight columns, a few hundred words"))
        adjT, adjT_parts = shared("adjT", [P, NT, N], "adjT_parts")
        probs, probs_parts = shared("probs", [P, NT, N], "probs_parts")
        wide, wide_parts = shared("wide", [P, 5672], "wide_parts")
        xres, scratch_parts = shared("xres", [P, NT, D], "scratch_parts")
        h = sb("h", [P, NT, D])
        y, y_parts = shared("y", [P, NT, D], "y_parts")
        hT = sb("hT", [P, C, N])
        gT, gT_parts = shared("gT", [P, 2 * NT * P], "gT_parts")
        wb1 = sb("wb1", [P, C, 2 * D])
        wb2 = sb("wb2", [P, C, 2 * D + 5])
        rowv = sb("rowv", [P, 3, D])
        part = sb("part", [P, 2, D])
        w13 = sb("w13", [P, C, 3 * A])
        w2s = sb("w2s", [A, 2 * A])
        ident = sb("ident", [P, P])
        ident_parts = sb("ident_parts", [P, P], F32R)
        waste = sb("waste", [P, N], BF16)
        stat = sb("stat", [P, 43, NT])
        bn6 = sb("bn6", [P, 6])
        top8 = sb("top8", [P, 2, NT, 8])
        cols = sb("cols", [P, 16])
        sq32 = sb("sq32", [P, 2, 32])
        flag = sb("flag", [1, 8])
        ones = sb("ones", [P, 1], BF16)
        flag_i = sb("flag_i", [1, 2], I32)
        gates = sb("gates", [P, NT, 2])
        gpre = sb("gpre", [P, NT, 3])
        ps = ctx.enter_context(nc.psum_tensor("ps", [P, 8, BANK], F32))
        psf = ps[:].rearrange("p b n -> p (b n)")
        x2_dram = nc.dram_tensor("x2_rows", (N, D), F32).ap()

        yflat = y[:].rearrange("p t n -> p (t n)")
        v0 = wide[:, 0:NT * (D + 2)].rearrange("p (t n) -> p t n", n=D + 2)
        hh1 = wide[:, NT * (D + 2):NT * (2 * D + 3)].rearrange("p (t n) -> p t n", n=D + 1)
        fb = wide[:, 0:NT * 2 * D].rearrange("p (t n) -> p t n", n=2 * D)
        x3 = wide[:, 0:NT * D].rearrange("p (t n) -> p t n", n=D)
        scratch = xres[:].rearrange("p t n -> p (t n)")
        masked = scratch[:, 0:N]
        dumps = (masked, scratch[:, N:2 * N], gT[:, 0:N])
        qT = scratch[0:A, 0:N]
        other = (waste, scratch[:, N:N + N // 2].bitcast(BF16))
        order = scratch[:, N + N // 2:2 * N].bitcast(F16)
        late = scratch[:, N + N // 2:2 * N].bitcast(BF16)
        left = gT[:, 0:N]
        adj_high = probs_parts[:].rearrange("p (t n) -> p t n", t=NT)
        adj_low = adjT_parts[:].rearrange("p (t n) -> p t n", t=NT)
        v_high = y_parts[:].rearrange("p (t n) -> p t n", t=NT)
        v_low = wide_parts[:, NT * D:2 * NT * D].rearrange("p (t n) -> p t n", t=NT)
        qw_parts = gT_parts[:, 0:N]
        k_high = gT_parts[:, N:2 * N]
        k_low = scratch_parts[:, N:2 * N]
        sxT = yflat.rearrange("p (t c n) -> p t c n", t=NT, c=C)
        pT = gT[:].rearrange("p (s t n) -> p s t n", s=2, t=NT)
        wsaT = yflat[:, 0:C * D].rearrange("p (c n) -> p c n", c=C)
        w_left = yflat[:, C * D:C * D + C * P].rearrange("p (c n) -> p c n", c=C)
        xa_row = part
        wl3 = wb2[:, 1, 0:2 * D].rearrange("p (s n) -> p s n", s=2)

        names = ("mean var std rstd shift rowsum col0 col1 col2 rinv cinv dnode zsum nmax least "
                 "lo mhi hi mlo goal probe mass under reached missed s1 s2 w1 w2 f1 f2 tstar allow kept kinv above open dinv "
                 "spred ssum scount tneg nudge").split()
        S = {n: stat[:, i, :] for i, n in enumerate(names)}

        def pair(first):
            return stat[:, names.index(first):names.index(first) + 2, :]

        lo_mhi, hi_mlo, probe_mass, mass_under, verdicts, chosen, gaps = map(
            pair, "lo hi probe mass reached s1 w1".split())
        goal_mass = stat[:, names.index("goal"):names.index("mass") + 1:2, :]

        x_in = [sem(f"x_in{g}") for g in range(len(GROUPS))]
        adj_in = [sem(f"adj_in{t}") for t in range(NT)]
        l0_in = sem("l0_in")
        l1_in = sem("l1_in")
        l2_in = sem("l2_in")
        u12_in = sem("u12_in")
        u12b_in = sem("u12b_in")
        u3_in = sem("u3_in")
        w3_in = sem("w3_in")
        vec_in = sem("vec_in")
        x2_out = sem("x2_out")
        x2_in = sem("x2_in")
        y_out = sem("y_out")
        ident_ready = sem("ident_ready")
        ones_set = sem("ones_set")
        stats_set = sem("stats_set")
        scale_ready = sem("scale_ready")
        std_ready = sem("std_ready")
        rstd_ready = sem("rstd_ready")
        h_ready = sem("h_ready")
        rows_turned = sem("rows_turned")
        hT_ready = sem("hT_ready")
        adj_turned = sem("adj_turned")
        adjT_ready = sem("adjT_ready")
        wd_ready = sem("wd_ready")
        hw_made = sem("hw_made")
        hw_taken = sem("hw_taken")
        v_made = sem("v_made")
        v_taken = sem("v_taken")
        bias_added = sem("bias_added")
        l0_made = sem("l0_made")
        l0_taken = sem("l0_taken")
        wsa_turned = sem("wsa_turned")
        wsaT_ready = sem("wsaT_ready")
        wlr_made = sem("wlr_made")
        wlr_ready = sem("wlr_ready")
        left_made = sem("left_made")
        left_ready = sem("left_ready")
        hh_made = sem("hh_made")
        hh_taken = sem("hh_taken")
        xg_made = sem("xg_made")
        xg_taken = sem("xg_taken")
        score_ready = sem("score_ready")
        leaky_ready = sem("leaky_ready")
        exp1_ready = sem("exp1_ready")
        attn_ready = sem("attn_ready")
        xb_made = sem("xb_made")
        xb_taken = sem("xb_taken")
        gates_pre = sem("gates_pre")
        gates_ready = sem("gates_ready")
        xa_made = sem("xa_made")
        mix_ready = sem("mix_ready")
        sig_ready = sem("sig_ready")
        x2_ready = sem("x2_ready")
        qk_made = sem("qk_made")
        qk_taken = sem("qk_taken")
        high_ready = sem("high_ready")
        logits_made = sem("logits_made")
        nmax_ready = sem("nmax_ready")
        exp_ready = sem("exp_ready")
        sx_made = sem("sx_made")
        sx_taken = sem("sx_taken")
        gu_made = sem("gu_made")
        gu_taken = sem("gu_taken")
        part_ready = sem("part_ready")
        part_added = sem("part_added")
        x_added = sem("x_added")
        masked_ready = sem("masked_ready")
        threshold_ready = sem("threshold_ready")
        other_ready = sem("other_ready")
        p_turned = sem("p_turned")
        pT_ready = sem("pT_ready")
        ax_made = sem("ax_made")
        ax_taken = sem("ax_taken")
        ax_added = sem("ax_added")
        xa_turned = sem("xa_turned")
        xaT_ready = sem("xaT_ready")
        xu_made = sem("xu_made")
        xu_taken = sem("xu_taken")
        sfb_made = sem("sfb_made")
        w3_turned = sem("w3_turned")
        w3T_ready = sem("w3T_ready")
        x2_biased = sem("x2_biased")
        norm_ready = sem("norm_ready")
        x3_ready = sem("x3_ready")
        adj_high_ready = sem("adj_high_ready")
        adj_low_ready = sem("adj_low_ready")
        ident_split = sem("ident_split")
        v3_made = sem("v3_made")
        v3_taken = sem("v3_taken")
        l3_made = sem("l3_made")
        l3_taken = sem("l3_taken")
        d_ready = sem("d_ready")
        dnode_ready = sem("dnode_ready")
        out_ready = sem("out_ready")
        dve_step = sem("dve_step")
        act_step = sem("act_step")
        pool_step = sem("pool_step")
        probe_ready = sem("probe_ready")
        share_ready = sem("share_ready")
        verify_step = [sem(f"verify_step{s}") for s in range(STEPS)]
        more_step = [sem(f"more_step{s}") for s in range(STEPS)]
        full_step = [sem(f"full_step{s}") for s in range(STEPS)]

        class Chain:

            def __init__(self, eng, own):
                self.eng, self.own, self.counts, self.base = eng, own, {}, None

            def link(self, ins):
                n = self.counts[self.own] = self.counts.get(self.own, 0) + 1
                ins.then_inc(self.own, 1)
                self.eng.wait_ge(self.own, n if self.base is None else self.base + n)

            def lag(self, ins):
                n = self.counts[self.own] = self.counts.get(self.own, 0) + 1
                ins.then_inc(self.own, 1)
                if n > 1:
                    self.eng.wait_ge(self.own, n - 1 if self.base is None else self.base + (n - 1))

            def tell(self, ins, other):
                n = self.counts[other] = self.counts.get(other, 0) + 1
                ins.then_inc(other, 1)
                self.eng.wait_ge(other, n)

        adj_rows = [adj[t * P:t * P + rows(t), :] for t in range(NT)]

        Q_BANKS, K_BANKS = (0, 1, 6), (2, 3, 7)
        V3_BANKS = (0, 1, 2, 3, 0, 1, 2, 3, 0, 1, 0)
        L3_BANKS = (2, 3, 6, 7, 0, 1, 4, 5)

        def turn_bank(g, c):
            return 4 + 2 * (g % 2) + c

        def out_bank(m):
            return 5 + m % 2

        def row_tiles(dram):
            full = (NT - 1) * P
            return (dram[0:full, :].rearrange("(t p) d -> p t d", p=P), dram[full:N, :])

        def chunks(w):
            return w.rearrange("(c p) n -> p c n", p=P)

        def bcast(v):
            return v.partition_broadcast(P)

        block = ctx.enter_context(nc.Block())

        @block.sync
        def _(sp):
            xm, xt = row_tiles(x)
            for g, group in enumerate(GROUPS):
                full = [t for t in group if rows(t) == P]
                some = slice(full[0], full[-1] + 1)
                sp.dma_start(xres[:, some, :], xm[:, some, :]).then_inc(x_in[g], 16)
                if len(full) < len(group):
                    sp.dma_start(xres[0:TAIL, NT - 1, :], xt).then_inc(x_in[g], 16)
            for t in range(NT):
                sp.dma_start(probs[0:rows(t), t, :], adj_rows[t]).then_inc(adj_in[t], 16)
            sp.dma_start(wb2[:, :, 0:D], chunks(w_sa)).then_inc(l1_in, 16)
            sp.dma_start(wb2[:, :, D:2 * D], chunks(w_gcnb)).then_inc(l1_in, 16)
            for k, w in enumerate((wa, wb)):
                for s in range(2):
                    sp.dma_start(wb2[:, :, 2 * D + k + 2 * s],
                                  w[0, s * D:(s + 1) * D].rearrange("(c p) -> p c", p=P)).then_inc(l1_in, 16)
            for s in range(2):
                sp.dma_start(cols[:, s:2 * C:2],
                              a_sa[0, s * D:(s + 1) * D].rearrange("(c p) -> p c", p=P)).then_inc(l1_in, 16)
            sp.dma_start(rowv[:, 1, :], bcast(b_gcnb)).then_inc(l1_in, 16)
            sp.dma_start(cols[:, 8:9], bcast(ba)).then_inc(l1_in, 16)
            sp.dma_start(cols[:, 9:10], bcast(bb)).then_inc(l1_in, 16)
            sp.dma_start(w13[:, :, 0:A], chunks(w1)).then_inc(l2_in, 16)
            for s in range(2):
                sp.dma_start(w13[:, :, (1 + s) * A:(2 + s) * A], chunks(w3)).then_inc(l2_in, 16)
                sp.dma_start(w2s[:, s * A:(s + 1) * A], w2).then_inc(l2_in, 16)
            sp.wait_ge(v_taken, NT)
            for k, u in enumerate((u1, u2)):
                sp.dma_start(wb1[:, :, k * D:(k + 1) * D], chunks(u[0])).then_inc(u12_in, 16)
            sp.wait_ge(hh_made, NT)
            for k, u in enumerate((u1, u2)):
                sp.dma_start(wb2[:, :, k * D:(k + 1) * D], chunks(u[1])).then_inc(u12b_in, 16)
            for t in range(NT):
                sp.wait_ge(x2_ready, t + 1)
                sp.dma_start(x2_dram[t * P:t * P + rows(t), :], xres[0:rows(t), t, :]).then_inc(x2_out, 16)
            sp.wait_ge(gu_made, 2 * NT)
            for s in range(STEPS):
                sp.dma_start(wb1[:, :, s * D:(s + 1) * D], chunks(u3[s])).then_inc(u3_in, 16)
            sp.dma_start(wl3, chunks(w_l3)).then_inc(w3_in, 16)
            sp.wait_ge(x2_ready, NT)
            for k, v in enumerate((gamma, beta, b_l3)):
                sp.dma_start(rowv[:, k, :], bcast(v)).then_inc(vec_in, 16)
            sp.wait_ge(sfb_made, NT)
            sp.wait_ge(x2_out, 16 * NT)
            xm, xt = row_tiles(x2_dram)
            sp.dma_start(x3[:, 0:NT - 1, :], xm).then_inc(x2_in, 16)
            sp.dma_start(x3[0:TAIL, NT - 1, :], xt).then_inc(x2_in, 16)
            for t in range(NT):
                sp.wait_ge(out_ready, t + 1)
                sp.dma_start(out[t * P:t * P + rows(t), :], xres[0:rows(t), t, :]).then_inc(y_out, 16)
            sp.wait_ge(y_out, 16 * NT)

        @block.gpsimd
        def _(pool):
            ch = Chain(pool, pool_step)
            ch.link(nc.gpsimd.memset(ident[:], 0.0))
            ch.tell(nc.gpsimd.affine_select(out=ident[:], in_=ident[:], compare_op=ALU.not_equal, fill=1.0,
                                            base=0, pattern=[[-1, P]], channel_multiplier=1), ident_ready)
            ch.tell(nc.gpsimd.memset(v0[:, :, D:D + 1], 1.0), ones_set)
            ch.tell(nc.gpsimd.memset(hh1[:, :, D:D + 1], 1.0), ones_set)
            pool.wait_ge(l0_in, 16 * 3)
            pool.wait_ge(h_ready, NT)
            for t in range(NT):
                r = rows(t)
                ch.tell(nc.gpsimd.tensor_tensor(xres[0:r, t, :], xres[0:r, t, :], rowv[0:r, 0, :], ALU.add),
                        bias_added)

            def add_part(n, t):
                r = rows(t)
                pool.wait_ge(part_ready, n + 1)
                ch.tell(nc.gpsimd.tensor_tensor(y[0:r, t, :], y[0:r, t, :], part[0:r, n % 2, :], ALU.add),
                        part_added)

            n = 0
            for t in range(NT):
                r = rows(t)
                add_part(n, t)
                n += 1
                ch.tell(nc.gpsimd.tensor_tensor(y[0:r, t, :], y[0:r, t, :], h[0:r, t, :], ALU.add), x_added)
            for t in range(NT):
                for _ in range(2):
                    add_part(n, t)
                    n += 1
            for t in range(NT):
                add_part(n, t)
                n += 1
            pool.wait_ge(x2_in, 32)
            pool.wait_ge(vec_in, 48)
            for t in range(NT):
                r = rows(t)
                ch.tell(nc.gpsimd.tensor_tensor(x3[0:r, t, :], x3[0:r, t, :], rowv[0:r, 1, :], ALU.add),
                        x2_biased)
            for t in range(NT):
                r = rows(t)
                pool.wait_ge(adj_high_ready, t + 1)
                ch.tell(nc.gpsimd.tensor_tensor(adj_low[0:r, t, :], adjT[0:r, t, :], adj_high[0:r, t, :],
                                                ALU.subtract), adj_low_ready)

        @block.tensor
        def _(pe):
            def bank(b, r, n, at=0):
                return ps[0:r, b, at:at + n]

            def product(dst, pairs):
                for k, (lhsT, rhs) in enumerate(pairs):
                    last = pe.matmul(dst, lhsT, rhs, start=(k == 0), stop=(k == len(pairs) - 1))
                return last

            def turn_rows(k, g):
                group = GROUPS[g]
                pe.wait_ge(h_ready, NT * k + group[-1] + 1)
                if g == 2:
                    pe.wait_ge(hT_ready, 6 * k + 2)
                for c in range(C):
                    for q, t in enumerate(group):
                        r = rows(t)
                        last = pe.transpose(bank(turn_bank(g, c), P, r, q * P), h[0:r, t, c * P:(c + 1) * P],
                                            ident[0:r, 0:r])
                    last.then_inc(rows_turned, 1)

            def adj_pairs(it, rhs, lhs=adjT, n=None):
                r = rows(it)
                return [(lhs[0:rows(jt), jt, it * P:it * P + r], rhs[0:rows(jt), jt, 0:n]) for jt in range(NT)]

            pe.wait_ge(ident_ready, 1)
            for g in range(len(GROUPS)):
                turn_rows(0, g)
            pe.wait_ge(wd_ready, 1)
            pe.wait_ge(hT_ready, 6)
            for t in range(NT):
                r, b = rows(t), 2 * (t % 3)
                hs = [hT[:, c, t * P:t * P + r] for c in range(C)]
                if t >= 3:
                    pe.wait_ge(hw_taken, t - 2)
                product(bank(b, r, D), [(hs[c], wb1[:, c, 0:D]) for c in range(C)]).then_inc(hw_made, 1)
                if t >= 3:
                    pe.wait_ge(v_taken, t - 2)
                product(bank(b + 1, r, D), [(hs[c], wb1[:, c, D:2 * D]) for c in range(C)]).then_inc(v_made, 1)
            ring = [6, 7, 0, 1, 2, 3, 4, 5]
            n = 0
            for group in GROUPS:
                for jt in range(NT):
                    if jt == 0:
                        for t in group:
                            pe.wait_ge(adj_in[t], 16)
                    if n == 2:
                        pe.wait_ge(hw_taken, NT)
                        pe.wait_ge(v_taken, NT)
                    if n >= 8:
                        pe.wait_ge(adjT_ready, n - 7)
                    for q, t in enumerate(group):
                        r = rows(t)
                        last = pe.transpose(bank(ring[n % 8], rows(jt), r, q * P),
                                            probs[0:r, t, jt * P:jt * P + rows(jt)], ident[0:r, 0:r])
                    last.then_inc(adj_turned, 1)
                    n += 1
            pe.wait_ge(adjT_ready, n)
            pe.wait_ge(v_taken, NT)
            pe.wait_ge(hw_taken, NT)
            pe.wait_ge(ones_set, 2)
            def left_scores(g):
                pe.wait_ge(hT_ready, 6 + 2 * g + 2)
                q, w = SLICES[g]
                product(bank(turn_bank(g, 0), P, w), [(w_left[:, c, :], hT[:, c, q:q + w]) for c in range(C)]
                        ).then_inc(left_made, 1)

            def layer1_rows(tiles):
                for t in tiles:
                    r, b = rows(t), 2 * (t % 2)
                    hs = [hT[:, c, t * P:t * P + r] for c in range(C)]
                    if t >= 2:
                        pe.wait_ge(xg_taken, t - 1)
                    product(bank(b + 1, r, D + 5), [(hs[c], wb2[:, c, D:2 * D + 5]) for c in range(C)]
                            ).then_inc(xg_made, 1)
                    if t >= 2:
                        pe.wait_ge(hh_taken, t - 1)
                    product(bank(b, r, D), [(hs[c], wb2[:, c, 0:D]) for c in range(C)]).then_inc(hh_made, 1)

            for it in range(NT):
                if it >= 4:
                    pe.wait_ge(l0_taken, it - 3)
                product(bank(it % 4, rows(it), D + 1), adj_pairs(it, v0, n=D + 1)).then_inc(l0_made, 1)
                if it == 0:
                    pe.wait_ge(l1_in, 16 * 11)
                    for e in range(C):
                        for c in range(C):
                            last = pe.transpose(bank(6, P, P, e * D + c * P), wb2[:, c, e * P:(e + 1) * P], ident[:])
                    last.then_inc(wsa_turned, 1)
                if it == 2:
                    pe.wait_ge(wsaT_ready, 1)
                    for c in range(C):
                        last = product(bank(7, P, 2, 2 * c),
                                       [(wsaT[:, e, c * P:(c + 1) * P], cols[:, 2 * e:2 * e + 2]) for e in range(C)])
                    last.then_inc(wlr_made, 1)
                if it == 7:
                    pe.wait_ge(wlr_ready, 1)
                    turn_rows(1, 0)
                if it == 8:
                    left_scores(0)
            turn_rows(1, 1)
            pe.wait_ge(l0_taken, NT)
            layer1_rows(GROUPS[0])
            left_scores(1)
            layer1_rows(GROUPS[1])
            pe.wait_ge(left_ready, 1)
            turn_rows(1, 2)
            left_scores(2)
            layer1_rows(GROUPS[2])
            pe.wait_ge(xg_taken, NT)
            pe.wait_ge(hh_taken, NT)
            pe.wait_ge(left_ready, 3)
            for it in range(NT):
                if it >= 8:
                    pe.wait_ge(xb_taken, it - 7)
                product(bank(it % 8, rows(it), D + 2), adj_pairs(it, v0, n=D + 2)).then_inc(xb_made, 1)
            pe.wait_ge(xb_taken, NT)
            pe.wait_ge(attn_ready, NT)
            for it in range(NT):
                if it >= 4:
                    pe.wait_ge(mix_ready, it - 3)
                product(bank(it % 4, rows(it), D + 1), adj_pairs(it, hh1, lhs=probs, n=D + 1)).then_inc(xa_made, 1)
                if it == 7:
                    turn_rows(2, 0)

            def project(g):
                q, n = SLICES[g]
                for w, b in ((w13[:, :, 0:A], Q_BANKS[g]), (w13[:, :, A:3 * A], K_BANKS[g])):
                    product(bank(b, w.shape[-1], n), [(w[:, c, :], hT[:, c, q:q + n]) for c in range(C)]
                            ).then_inc(qk_made, 1)

            def logits(step):
                for k, (s, n) in enumerate(SLICES):
                    pe.wait_ge(qk_taken, 9 * step + 2 * k + 1)
                    product(bank(Q_BANKS[k], 2 * A, n), [(w2s[:], qT[:, s:s + n])]).then_inc(qk_made, 1)
                pe.wait_ge(qk_taken, 9 * step + 9)
                for it in range(NT):
                    if it >= 2:
                        pe.wait_ge(nmax_ready, NT * step + it - 1)
                    for k, (s, n) in enumerate(SLICES):
                        qs = qw_parts[:, it * P:it * P + rows(it)]
                        last = product(bank(4 * (it % 2) + k, rows(it), n),
                                       [(qs, k_high[:, s:s + n]), (qs, k_low[:, s:s + n])])
                    last.then_inc(logits_made, 1)
                pe.wait_ge(nmax_ready, NT * (step + 1))

            def turn_weights(step, t):
                r = rows(t)
                m = step * NT + t
                pe.wait_ge(masked_ready, m + 1)
                for g, group in enumerate(GROUPS):
                    job = 3 * m + g
                    if job >= 5:
                        pe.wait_ge(pT_ready, job - 4)
                    for q, jt in enumerate(group):
                        last = pe.transpose(bank(job % 5, rows(jt), r, q * P),
                                            probs[0:r, t, jt * P:jt * P + rows(jt)], ident[0:r, 0:r])
                    last.then_inc(p_turned, 1)

            def turn_xa(t):
                r = rows(t)
                pe.wait_ge(ax_taken, t + 1)
                if t >= 1:
                    pe.wait_ge(xaT_ready, t)
                for c in range(C):
                    last = pe.transpose(bank(7, P, r, c * P), xa_row[0:r, t % 2, c * P:(c + 1) * P],
                                        ident[0:r, 0:r])
                last.then_inc(xa_turned, 1)

            def weights_times(step):
                turn_weights(step, 0)
                for t in range(NT):
                    r = rows(t)
                    m = step * NT + t
                    if t < NT - 1:
                        turn_weights(step, t + 1)
                    pe.wait_ge(pT_ready, 3 * m + 3)
                    if m >= NT + 2:
                        pe.wait_ge(ax_added, t - 1)
                    elif m >= 2:
                        pe.wait_ge(ax_taken, min(m - 1, NT))
                    product(bank(out_bank(m), r, D), [(pT[0:rows(jt), m % 2, jt, 0:r], h[0:rows(jt), jt, :])
                                                      for jt in range(NT)]).then_inc(ax_made, 1)
                    if step == 0 and t >= 1:
                        turn_xa(t - 1)
                if step == 0:
                    turn_xa(NT - 1)

            pe.wait_ge(mix_ready, NT)
            pe.wait_ge(l2_in, 16 * 5)
            turn_rows(2, 1)
            pe.wait_ge(hT_ready, 14)
            project(0)
            pe.wait_ge(hT_ready, 16)
            project(1)
            turn_rows(2, 2)
            pe.wait_ge(hT_ready, 18)
            project(2)
            logits(0)
            for jt in range(NT):
                r = rows(jt)
                for c in range(C):
                    xs = h[0:r, jt, c * P:(c + 1) * P]
                    for k, (s, n) in enumerate(SLICES):
                        pe.matmul(bank(3 * c + k, P, n), xs, adjT[0:r, jt, s:s + n], start=(jt == 0), stop=False)
            for c in range(C):
                for k, (s, n) in enumerate(SLICES):
                    pe.matmul(bank(3 * c + k, P, n), ident[:], hT[:, c, s:s + n],
                              start=False, stop=True).then_inc(sx_made, 1)
            pe.wait_ge(sx_taken, 2 * len(SLICES))
            pe.wait_ge(u12_in, 32)
            pe.wait_ge(u12b_in, 32)

            def sx_times_u(tiles):
                for t in tiles:
                    r = rows(t)
                    for k, w in enumerate((wb1, wb2)):
                        if t >= 2:
                            pe.wait_ge(gu_taken, t - 1)
                        product(bank((2 * t + k) % 4, r, 2 * D),
                                [(sxT[:, t, c, 0:r], w[:, c, 0:2 * D]) for c in range(C)]).then_inc(gu_made, 1)

            sx_times_u(range(GU_EARLY))
            pe.wait_ge(gu_taken, GU_EARLY)
            weights_times(0)
            pe.wait_ge(xaT_ready, NT)
            for g in range(len(GROUPS)):
                project(g)
            logits(1)
            sx_times_u(range(GU_EARLY, NT))
            pe.wait_ge(gu_taken, NT)
            for it in range(NT):
                r = rows(it)
                if it >= 4:
                    pe.wait_ge(part_ready, NT + 2 * (it - 3))
                product(bank(it % 4, r, 2 * D), adj_pairs(it, fb, n=2 * D) +
                        [(ident[0:r, 0:r], fb[0:r, it, :])]).then_inc(sfb_made, 1)
            pe.wait_ge(u3_in, 32)
            pe.wait_ge(part_ready, 3 * NT)
            for t in range(NT):
                r = rows(t)
                if t >= 4:
                    pe.wait_ge(xu_taken, t - 3)
                product(bank(t % 4, r, 2 * D),
                        [(hT[:, c, t * P:t * P + r], wb1[:, c, :]) for c in range(C)]).then_inc(xu_made, 1)
            pe.wait_ge(w3_in, 16)
            for e in range(C):
                for c in range(C):
                    last = pe.transpose(bank(4, P, P, c * D + e * P), wl3[:, e, c * P:(c + 1) * P], ident[:])
            last.then_inc(w3_turned, 1)
            pe.wait_ge(xu_taken, NT)
            pe.wait_ge(w3T_ready, 1)
            weights_times(1)

            def layer3_rows(tiles):
                for t in tiles:
                    r = rows(t)
                    if 4 <= t < 8:
                        pe.wait_ge(v3_taken, t - 3)
                    if t == NT - 1:
                        pe.wait_ge(v3_taken, t - 1)
                    product(bank(V3_BANKS[t], r, D), [(hT[:, c, t * P:t * P + r], wb1[:, c, 0:D]) for c in range(C)]
                            ).then_inc(v3_made, 1)

            def layer3_sum(it, jts, first, last):
                r, b = rows(it), L3_BANKS[it % 8]
                pairs = []
                for jt in jts:
                    cut = (slice(0, rows(jt)), jt, slice(it * P, it * P + r))
                    v = (slice(0, rows(jt)), jt)
                    pairs += [(adj_high[cut], v_high[v]), (adj_high[cut], v_low[v]), (adj_low[cut], v_high[v])]
                if last:
                    pairs += [(ident_parts[0:r, 0:r], v_high[0:r, it, :]), (ident_parts[0:r, 0:r], v_low[0:r, it, :])]
                for k, (lhsT, rhs) in enumerate(pairs):
                    ins = pe.matmul(bank(b, r, D), lhsT, rhs, start=(first and k == 0),
                                    stop=(last and k == len(pairs) - 1))
                if last:
                    ins.then_inc(l3_made, 1)

            pe.wait_ge(ax_added, NT - 1)
            turn_rows(3, 0)
            pe.wait_ge(hT_ready, 20)
            layer3_rows(GROUPS[0])
            pe.wait_ge(ax_added, NT)
            turn_rows(3, 1)
            pe.wait_ge(hT_ready, 22)
            layer3_rows(GROUPS[1])
            early = range(0, GROUPS[1][-1] + 1)
            pe.wait_ge(v3_taken, early[-1] + 1)
            pe.wait_ge(ident_split, 1)
            pe.wait_ge(adj_low_ready, early[-1] + 1)
            for it in range(4):
                layer3_sum(it, early, True, False)
            turn_rows(3, 2)
            pe.wait_ge(hT_ready, 24)
            layer3_rows(GROUPS[2])
            pe.wait_ge(v3_taken, NT)
            pe.wait_ge(adj_low_ready, NT)
            for it in range(4):
                layer3_sum(it, GROUPS[2], False, True)
            for it in range(4, NT):
                if it >= 8:
                    pe.wait_ge(l3_taken, it - 7)
                layer3_sum(it, range(NT), True, True)

        @block.scalar
        def _(act):
            ch = Chain(act, act_step)
            act.dma_start(wb1[:, :, 0:D], chunks(w0)).then_inc(l0_in, 16)
            act.dma_start(cols[:, 6:6 + C], diag1.rearrange("(c p) -> p c", p=P)).then_inc(l0_in, 16)
            act.dma_start(rowv[:, 0, :], bcast(bias0)).then_inc(l0_in, 16)

            def norm_root(g):
                some = slice(GROUPS[g][0], GROUPS[g][-1] + 1)
                act.wait_ge(scale_ready, ch.counts.get(std_ready, 0) + 1)
                ch.tell(nc.scalar.activation(S["std"][:, some], S["var"][:, some], ACT.Sqrt, bias=cols[:, 10:11]),
                        std_ready)

            def norm_apply(g, dst, src, func, done, free=None):
                act.wait_ge(rstd_ready, ch.counts[std_ready])
                if free is not None:
                    act.wait_ge(*free)
                for t in GROUPS[g]:
                    r = rows(t)
                    ch.tell(nc.scalar.activation(dst[0:r, t, :], src[0:r, t, :], func,
                                                 bias=S["shift"][0:r, t:t + 1], scale=S["rstd"][0:r, t:t + 1]), done)

            def norm_rows(g, *args, **kwargs):
                norm_root(g)
                norm_apply(g, *args, **kwargs)

            for g in range(len(GROUPS)):
                norm_rows(g, h, xres, ACT.Relu, h_ready)
            act.wait_ge(ones_set, 1)
            for t in range(NT):
                r = rows(t)
                act.wait_ge(v_made, t + 1)
                ch.tell(nc.scalar.copy(v0[0:r, t, 0:D], ps[0:r, 2 * (t % 3) + 1, 0:D]), v_taken)
            ring = [6, 7, 0, 1, 2, 3, 4, 5]
            n = 0
            for g, group in enumerate(GROUPS):
                w = width(group)
                for jt in range(NT):
                    r = rows(jt)
                    act.wait_ge(adj_turned, n + 1)
                    ch.tell(nc.scalar.activation(adjT[0:r, jt, g * BANK:g * BANK + w], ps[0:r, ring[n % 8], 0:w],
                                                 ACT.Copy, accum_out=S[f"col{g}"][0:r, jt:jt + 1]), adjT_ready)
                    n += 1
            def take_left(g):
                q, w = SLICES[g]
                act.wait_ge(left_made, g + 1)
                ch.tell(nc.scalar.copy(left[:, q:q + w], ps[:, turn_bank(g, 0), 0:w]), left_ready)

            def take_hh(tiles):
                for t in tiles:
                    r = rows(t)
                    act.wait_ge(hh_made, t + 1)
                    ch.tell(nc.scalar.copy(hh1[0:r, t, 0:D], ps[0:r, 2 * (t % 2), 0:D]), hh_taken)

            norm_rows(0, h, xres, ACT.Relu, h_ready)
            norm_rows(1, h, xres, ACT.Relu, h_ready)
            take_left(0)
            norm_rows(2, h, xres, ACT.Relu, h_ready)
            take_hh(GROUPS[0])
            take_left(1)
            take_hh(GROUPS[1])
            take_left(2)
            take_hh(GROUPS[2])
            act.wait_ge(xg_taken, NT)
            for t in range(NT):
                r = rows(t)
                ch.tell(nc.scalar.activation(probs[0:r, t, :], left[0:r, :], ACT.Identity,
                                             bias=gpre[0:r, t, 2:3]), score_ready)
            for t in range(NT):
                r = rows(t)
                act.wait_ge(leaky_ready, t + 1)
                ch.tell(nc.scalar.activation(probs[0:r, t, :], probs[0:r, t, :], ACT.Exp, scale=-1.0), exp1_ready)
            act.wait_ge(gates_pre, 1)
            ch.tell(nc.scalar.activation(gates[:], gates[:], ACT.Sigmoid), gates_ready)
            for g, group in enumerate(GROUPS):
                for t in group:
                    r = rows(t)
                    act.wait_ge(mix_ready, t + 1)
                    ch.tell(nc.scalar.activation(y[0:r, t, :], y[0:r, t, :], ACT.Sigmoid), sig_ready)
                norm_rows(g, h, xres, ACT.Relu, h_ready)

            def softmax_rows(step):
                for k, (s, n) in enumerate(SLICES):
                    act.wait_ge(qk_made, 9 * step + 2 * k + 2)
                    ch.tell(nc.scalar.copy(k_high[:, s:s + n], ps[:, K_BANKS[k], 0:n]), high_ready)
                for k, (s, n) in enumerate(SLICES):
                    act.wait_ge(qk_made, 9 * step + 6 + k + 1)
                    ch.tell(nc.scalar.copy(qw_parts[:, s:s + n], ps[:, Q_BANKS[k], 0:n]), high_ready)
                for t in range(NT):
                    r = rows(t)
                    act.wait_ge(nmax_ready, NT * step + t + 1)
                    ch.tell(nc.scalar.activation(probs[0:r, t, :], probs[0:r, t, :], ACT.Exp,
                                                 bias=S["nmax"][0:r, t:t + 1], scale=-1.0,
                                                 accum_out=S["zsum"][0:r, t:t + 1]), exp_ready)

            def share_mass(n):
                act.wait_ge(probe_ready, n + 1)
                for t in range(NT - SHARED, NT):
                    r = rows(t)
                    limit = S["spred"][0:r, t:t + 1]
                    ch.link(nc.scalar.activation(waste[0:r, :], probs[0:r, t, :], ACT.Relu, bias=limit,
                                                 accum_out=S["ssum"][0:r, t:t + 1]))
                    ins = nc.scalar.activation(waste[0:r, :], waste[0:r, :], ACT.Sign,
                                               accum_out=S["scount"][0:r, t:t + 1])
                    if t < NT - 1:
                        ch.link(ins)
                    else:
                        ch.tell(ins, share_ready)

            parts = [0]

            def part_out(src, scale, r):
                n = parts[0]
                if n >= 2:
                    act.wait_ge(part_added, n - 1)
                ins = nc.scalar.activation(part[0:r, n % 2, :], src, ACT.Copy, scale=scale)
                parts[0] += 1
                return ins

            def mark_others(step, t):
                r = rows(t)
                buf = other[t % 2][0:r, :]
                if t == 0:
                    act.wait_ge(threshold_ready, step + 1)
                if t >= 2:
                    act.wait_ge(masked_ready, step * NT + t - 1)
                ch.link(nc.scalar.activation(buf, probs[0:r, t, :], ACT.Sign, bias=S["tneg"][0:r, t:t + 1]))
                ch.tell(nc.scalar.activation(buf, buf, ACT.Square), other_ready)

            def split_adj(t):
                r = rows(t)
                ch.tell(nc.scalar.copy(adj_high[0:r, t, :], adjT[0:r, t, :]), adj_high_ready)

            def turned_weights(step, t):
                r = rows(t)
                m = step * NT + t
                for g, group in enumerate(GROUPS):
                    job = 3 * m + g
                    act.wait_ge(p_turned, job + 1)
                    b = job % 5
                    if m >= 2 and g == 0:
                        act.wait_ge(ax_made, m - 1)
                    full = [jt for jt in group if rows(jt) == P]
                    k = len(full)
                    src = ps[:, b, 0:k * P].rearrange("p (q n) -> p q n", n=P)[:, :, 0:r]
                    ins = nc.scalar.copy(pT[:, m % 2, group[0]:group[0] + k, 0:r], src)
                    if k == len(group):
                        ch.tell(ins, pT_ready)
                    else:
                        ch.link(ins)
                        jt = group[-1]
                        ch.tell(nc.scalar.copy(pT[0:rows(jt), m % 2, jt, 0:r],
                                               ps[0:rows(jt), b, k * P:k * P + r]), pT_ready)

            softmax_rows(0)
            for k in range(1 + 2 * PAIRS[0]):
                share_mass(k)
            for c in range(C):
                for k, (s, n) in enumerate(SLICES):
                    act.wait_ge(sx_made, 3 * c + k + 1)
                    tiles = range(s // P, -(-(s + n) // P))
                    full = [t for t in tiles if rows(t) == P]
                    src = ps[:, 3 * c + k, 0:len(full) * P].rearrange("p (t n) -> p t n", n=P)
                    ins = nc.scalar.copy(sxT[:, full[0]:full[-1] + 1, c, :], src)
                    if len(full) < len(tiles):
                        ch.link(ins)
                        ins = nc.scalar.copy(sxT[:, NT - 1, c, 0:TAIL],
                                             ps[:, 3 * c + k, len(full) * P:len(full) * P + TAIL])
                    ch.tell(ins, sx_taken)

            def take_gu(t):
                r = rows(t)
                b = (2 * t) % 4
                dr, dc = S["rinv"][0:r, t:t + 1], S["cinv"][0:r, t:t + 1]
                act.wait_ge(gu_made, 2 * t + 2)
                ch.link(nc.scalar.activation(y[0:r, t, :], ps[0:r, b, 0:D], ACT.Copy, scale=dr))
                ch.tell(part_out(ps[0:r, b, D:2 * D], dc, r), part_ready)
                ch.link(nc.scalar.activation(fb[0:r, t, 0:D], ps[0:r, b + 1, 0:D], ACT.Copy, scale=dr))
                ch.tell(nc.scalar.activation(fb[0:r, t, D:2 * D], ps[0:r, b + 1, D:2 * D], ACT.Copy,
                                             scale=dc), gu_taken)

            for t in range(GU_EARLY):
                take_gu(t)
            act.wait_ge(part_added, GU_EARLY)
            mark_others(0, 0)
            mark_others(0, 1)
            turned_weights(0, 0)
            mark_others(0, 2)
            for t in range(NT + 1):
                if t < NT - 1:
                    turned_weights(0, t + 1)
                if t < NT - 3:
                    mark_others(0, t + 3)
                if t < NT:
                    r = rows(t)
                    act.wait_ge(ax_made, t + 1)
                    if t >= 2:
                        act.wait_ge(xa_turned, t - 1)
                    ch.tell(nc.scalar.activation(xa_row[0:r, t % 2, :], ps[0:r, out_bank(t), 0:D], ACT.Copy,
                                                 scale=S["kinv"][0:r, t:t + 1]), ax_taken)
                if t >= 1:
                    r, q = rows(t - 1), (t - 1) * P
                    act.wait_ge(xa_turned, t)
                    ch.tell(nc.scalar.copy(hT[:, :, q:q + r],
                                           ps[:, 7, 0:C * P].rearrange("p (c n) -> p c n", c=C)[:, :, 0:r]), xaT_ready)
            softmax_rows(1)

            def spread(k, among, tiles):
                if k not in among:
                    return tiles[0:0]
                k, n = k - among[0], len(among)
                return tiles[len(tiles) * k // n:len(tiles) * (k + 1) // n]

            probes = 1 + 2 * PAIRS[1]
            for k in range(probes):
                share_mass(1 + 2 * PAIRS[0] + k)
                for t in spread(k, GU_PROBES, range(GU_EARLY, NT)):
                    take_gu(t)
                for t in spread(k, SFB_PROBES, range(NT)):
                    r = rows(t)
                    dr, dc = S["rinv"][0:r, t:t + 1], S["cinv"][0:r, t:t + 1]
                    act.wait_ge(sfb_made, t + 1)
                    ch.tell(part_out(ps[0:r, t % 4, 0:D], dr, r), part_ready)
                    ch.tell(part_out(ps[0:r, t % 4, D:2 * D], dc, r), part_ready)
            for t in range(NT):
                r = rows(t)
                act.wait_ge(xu_made, t + 1)
                ch.tell(part_out(ps[0:r, t % 4, 0:D], 1.0, r), part_ready)
                act.wait_ge(x_added, t + 1)
                ch.tell(nc.scalar.copy(h[0:r, t, :], ps[0:r, t % 4, D:2 * D]), xu_taken)
            share_mass(1 + 2 * PAIRS[0] + probes)
            act.wait_ge(w3_turned, 1)
            ch.tell(nc.scalar.copy(wb1[:, :, 0:D], ps[:, 4, :].rearrange("p (c n) -> p c n", c=C)), w3T_ready)
            act.wait_ge(d_ready, 1)
            ch.tell(nc.scalar.activation(S["dnode"], S["dinv"], ACT.Sqrt), dnode_ready)
            mark_others(1, 0)
            mark_others(1, 1)
            ch.tell(nc.scalar.copy(ident_parts[:], ident[:]), ident_split)
            turned_weights(1, 0)
            mark_others(1, 2)
            for t in range(1, NT):
                turned_weights(1, t)
                if t < NT - 2:
                    mark_others(1, t + 2)
                split_adj(t - 1)
                for g in range(2):
                    if t == GROUPS[g][-1] + 2:
                        norm_root(g)
                    if t == GROUPS[g][-1] + 3:
                        norm_apply(g, y, y, ACT.Identity, norm_ready)
            split_adj(NT - 1)
            norm_rows(0, h, x3, ACT.Relu, h_ready, free=(ax_made, 2 * NT))
            norm_rows(2, y, y, ACT.Identity, norm_ready)
            norm_rows(1, h, x3, ACT.Relu, h_ready)
            norm_rows(2, h, x3, ACT.Relu, h_ready)

        @block.vector
        def _(dve):
            ch = Chain(dve, dve_step)
            V = nc.vector
            ch.link(V.memset(stat[:], 1.0))
            ch.link(V.memset(top8[:], 1.0))
            ch.link(V.memset(gates[:], 0.0))
            ch.link(V.memset(ones[:], 1.0))
            ch.link(V.memset(gpre[:], 0.0))
            ch.link(V.memset(cols[:, 10:11], LN_EPS))
            ch.link(V.memset(sq32[:], 0.0))

            def stats_of(src, t, finish=True):
                r = rows(t)
                ch.link(V.bn_stats(bn6[0:r, :], src))
                aggr = V.bn_aggr(stat[0:r, 0:2, t], bn6[0:r, :])
                for g, group in enumerate(GROUPS):
                    if t == group[-1]:
                        ch.tell(aggr, scale_ready)
                        if finish:
                            finish_stats(g)
                        return
                ch.link(aggr)

            def finish_stats(g):
                some = slice(GROUPS[g][0], GROUPS[g][-1] + 1)
                dve.wait_ge(std_ready, ch.counts[scale_ready])
                ch.link(V.reciprocal(S["rstd"][:, some], S["std"][:, some]))
                ch.tell(V.scalar_tensor_tensor(S["shift"][:, some], S["mean"][:, some], -1.0, S["rstd"][:, some],
                                               ALU.mult, ALU.mult), rstd_ready)

            def take_turned(k, g):
                w = width(GROUPS[g])
                for c in range(C):
                    dve.wait_ge(rows_turned, 6 * k + g * C + c + 1)
                    ch.tell(V.tensor_copy(hT[:, c, g * BANK:g * BANK + w], ps[:, turn_bank(g, c), 0:w]), hT_ready)

            for t in range(NT):
                for g, group in enumerate(GROUPS):
                    if t == group[0]:
                        dve.wait_ge(x_in[g], 32 if NT - 1 in group else 16)
                stats_of(xres[0:rows(t), t, :], t)
            dve.wait_ge(l0_in, 16 * 3)
            ch.link(V.tensor_scalar(cols[:, 6:6 + C], cols[:, 6:6 + C], 1.0, None, ALU.add))
            for c in range(C):
                ins = V.tensor_scalar(wb1[:, c, D:2 * D], wb1[:, c, 0:D], cols[:, 6 + c:7 + c], None, ALU.mult)
                if c < C - 1:
                    ch.link(ins)
                else:
                    ch.tell(ins, wd_ready)
            for g in range(len(GROUPS)):
                take_turned(0, g)
            for t in range(NT):
                r = rows(t)
                dve.wait_ge(hw_made, t + 1)
                dve.wait_ge(bias_added, t + 1)
                ch.tell(V.tensor_tensor(xres[0:r, t, :], xres[0:r, t, :], ps[0:r, 2 * (t % 3), 0:D], ALU.add),
                        hw_taken)
            for t in range(NT):
                r = rows(t)
                dve.wait_ge(l0_made, t + 1)
                ch.link(V.tensor_tensor(xres[0:r, t, :], xres[0:r, t, :], ps[0:r, t % 4, 0:D], ALU.subtract))
                ch.tell(V.tensor_copy(S["rowsum"][0:r, t:t + 1], ps[0:r, t % 4, D:D + 1]), l0_taken)
                stats_of(xres[0:r, t, :], t)
                if t == 0:
                    dve.wait_ge(wsa_turned, 1)
                    ch.tell(V.tensor_copy(wsaT, ps[:, 6, :].rearrange("p (c n) -> p c n", c=C)), wsaT_ready)
                if t == 2:
                    dve.wait_ge(wlr_made, 1)
                    for c in range(C):
                        ch.link(V.memset(w_left[:, c, :], 1.0))
                        ch.link(V.tensor_scalar(w_left[:, c, :], w_left[:, c, :], ps[:, 7, 2 * c:2 * c + 1], None,
                                                ALU.mult))
                        ins = V.tensor_copy(wb2[:, c, 2 * D + 4:2 * D + 5], ps[:, 7, 2 * c + 1:2 * c + 2])
                        if c < C - 1:
                            ch.link(ins)
                        else:
                            ch.tell(ins, wlr_ready)
                if t == 7:
                    take_turned(1, 0)

            def take_xg(tiles):
                for t in tiles:
                    r = rows(t)
                    dve.wait_ge(xg_made, t + 1)
                    b = 2 * (t % 2) + 1
                    ch.link(V.tensor_copy(v0[0:r, t, :], ps[0:r, b, 0:D + 2]))
                    ch.tell(V.tensor_copy(gpre[0:r, t, :], ps[0:r, b, D + 2:D + 5]), xg_taken)

            dve.wait_ge(l1_in, 16 * 11)
            take_turned(1, 1)
            take_xg(GROUPS[0])
            take_xg(GROUPS[1])
            take_turned(1, 2)
            take_xg(GROUPS[2])
            ch.link(V.tensor_scalar(S["rinv"], S["rowsum"], 1.0, 1e-12, ALU.add, ALU.max))
            ch.link(V.reciprocal(S["rinv"], S["rinv"]))
            ch.link(V.tensor_tensor(S["cinv"], S["col0"], S["col1"], ALU.add))
            ch.link(V.tensor_tensor(S["cinv"], S["cinv"], S["col2"], ALU.add))
            ch.link(V.tensor_scalar(S["cinv"], S["cinv"], 1.0, 1e-12, ALU.add, ALU.max))
            ch.link(V.reciprocal(S["cinv"], S["cinv"]))
            ch.link(V.tensor_scalar(S["dinv"], S["rowsum"], 1.0, None, ALU.add))
            ch.tell(V.reciprocal(S["dinv"], S["dinv"]), d_ready)
            for t in range(NT):
                row = probs[0:rows(t), t, :]
                dve.wait_ge(score_ready, t + 1)
                ch.tell(V.scalar_tensor_tensor(row, row, SLOPE, row, ALU.mult, ALU.max), leaky_ready)
            for t in range(NT):
                r = rows(t)
                dve.wait_ge(exp1_ready, t + 1)
                ch.tell(V.scalar_tensor_tensor(probs[0:r, t, :], adjT[0:r, t, :], 0.0, probs[0:r, t, :],
                                               ALU.not_equal, ALU.mult), attn_ready)
            for t in range(NT):
                r = rows(t)
                dve.wait_ge(xb_made, t + 1)
                ch.link(V.tensor_tensor(y[0:r, t, :], ps[0:r, t % 8, 0:D], rowv[0:r, 1, :], ALU.add))
                ch.tell(V.tensor_tensor(gates[0:r, t, :], ps[0:r, t % 8, D:D + 2], gpre[0:r, t, 0:2], ALU.add),
                        xb_taken)
            ch.link(V.tensor_scalar(gates[:, :, 0], gates[:, :, 0], cols[:, 8:9], None, ALU.add))
            ch.tell(V.tensor_scalar(gates[:, :, 1], gates[:, :, 1], cols[:, 9:10], None, ALU.add), gates_pre)
            dve.wait_ge(gates_ready, 1)

            def mix(t):
                r = rows(t)
                dve.wait_ge(xa_made, t + 1)
                ratio = S["f1"][0:r, t:t + 1]
                ch.link(V.tensor_scalar(ratio, ps[0:r, t % 4, D:D + 1], SOFT_EPS, None, ALU.add))
                ch.link(V.reciprocal(ratio, ratio))
                ch.link(V.tensor_tensor(ratio, ratio, gates[0:r, t, 0:1], ALU.mult))
                ch.link(V.tensor_scalar(y[0:r, t, :], y[0:r, t, :], gates[0:r, t, 1:2], None, ALU.mult))
                ch.tell(V.scalar_tensor_tensor(y[0:r, t, :], ps[0:r, t % 4, 0:D], ratio, y[0:r, t, :],
                                               ALU.mult, ALU.add), mix_ready)

            def residual(t):
                r = rows(t)
                dve.wait_ge(sig_ready, t + 1)
                ch.tell(V.tensor_tensor(xres[0:r, t, :], xres[0:r, t, :], y[0:r, t, :], ALU.add), x2_ready)
                stats_of(xres[0:r, t, :], t)

            for t in range(NT + 1):
                if t < NT:
                    mix(t)
                if t >= 1:
                    residual(t - 1)
                if t == 8:
                    take_turned(2, 0)
            take_turned(2, 1)
            take_turned(2, 2)
            dve.wait_ge(x2_out, 16 * NT)

            def project_out(step):
                for k, (s, n) in enumerate(SLICES):
                    dve.wait_ge(qk_made, 9 * step + 2 * k + 1)
                    ch.tell(V.tensor_copy(qT[:, s:s + n], ps[0:A, Q_BANKS[k], 0:n]), qk_taken)
                    dve.wait_ge(high_ready, 6 * step + k + 1)
                    ch.tell(V.tensor_tensor(k_low[:, s:s + n], ps[:, K_BANKS[k], 0:n], k_high[:, s:s + n],
                                            ALU.subtract), qk_taken)
                for k, (s, n) in enumerate(SLICES):
                    dve.wait_ge(high_ready, 6 * step + 3 + k + 1)
                    low = qw_parts[A:P, s:s + n]
                    ch.tell(V.tensor_tensor(low, ps[A:P, Q_BANKS[k], 0:n], low, ALU.subtract), qk_taken)

            def maxima(step):
                for t in range(NT):
                    r = rows(t)
                    b = 4 * (t % 2) * BANK
                    dve.wait_ge(logits_made, NT * step + t + 1)
                    ch.tell(V.tensor_scalar(probs[0:r, t, :], psf[0:r, b:b + N], -1.0, None, ALU.mult, ALU.min,
                                            accum_out=S["nmax"][0:r, t:t + 1]), nmax_ready)

            def mass_above(c, limit, mass):
                for t in range(NT):
                    r = rows(t)
                    (c.link if t == NT - 1 else c.lag)(
                        V.scalar_tensor_tensor(dumps[t % 2][0:r, :], probs[0:r, t, :], limit[0:r, t:t + 1],
                                               probs[0:r, t, :], ALU.is_ge, ALU.mult,
                                               accum_out=mass[0:r, t:t + 1]))

            theirs = slice(NT - SHARED, NT)

            def show_limit(limit):
                V.tensor_scalar(S["spred"][:, theirs], limit[:, theirs], -BELOW, None, ALU.mult).then_inc(
                    probe_ready, 1)

            def mass_shared(c, limit, n):
                show_limit(limit)
                for t in range(NT - SHARED):
                    (c.link if t == NT - SHARED - 1 else c.lag)(
                        V.scalar_tensor_tensor(dumps[t % 2], probs[:, t, :], limit[:, t:t + 1], probs[:, t, :],
                                               ALU.is_ge, ALU.mult, accum_out=S["mass"][:, t:t + 1]))
                dve.wait_ge(share_ready, n + 1)
                c.link(V.tensor_tensor(S["scount"][:, theirs], S["scount"][:, theirs], S["spred"][:, theirs],
                                       ALU.mult))
                c.link(V.tensor_tensor(S["mass"][:, theirs], S["ssum"][:, theirs], S["scount"][:, theirs],
                                       ALU.subtract))

            def narrow(c, shared=None):
                if shared is None:
                    mass_above(c, S["probe"], S["mass"])
                else:
                    mass_shared(c, S["probe"], shared)
                c.link(V.tensor_tensor(verdicts, mass_under, goal_mass, ALU.is_ge))
                c.lag(V.tensor_tensor(chosen, probe_mass, verdicts, ALU.mult))
                c.lag(V.scalar_tensor_tensor(gaps, verdicts, HUGE, probe_mass, ALU.mult, ALU.max))
                c.lag(V.tensor_tensor(lo_mhi, lo_mhi, chosen, ALU.max))
                c.link(V.tensor_tensor(hi_mlo, hi_mlo, gaps, ALU.min))

            def midpoint(c):
                c.link(V.tensor_tensor(S["w1"], S["hi"], S["lo"], ALU.subtract))
                c.link(V.scalar_tensor_tensor(S["probe"], S["w1"], 0.5, S["lo"], ALU.mult, ALU.add))

            def interpolate(c):
                c.lag(V.tensor_tensor(gaps, hi_mlo, lo_mhi, ALU.subtract))
                c.link(V.scalar_tensor_tensor(S["f1"], S["lo"], AHEAD, S["mlo"], ALU.mult, ALU.add))
                c.link(V.tensor_tensor(S["f1"], S["f1"], S["goal"], ALU.subtract))
                c.link(V.reciprocal(S["f2"], S["w2"]))
                c.link(V.tensor_tensor(S["f1"], S["f1"], S["f2"], ALU.mult))
                c.link(V.tensor_scalar(S["f1"], S["f1"], CLIP_LO, CLIP_HI, ALU.max, ALU.min))
                c.link(V.tensor_tensor(S["f1"], S["f1"], S["w1"], ALU.mult))
                c.link(V.tensor_tensor(S["probe"], S["lo"], S["f1"], ALU.add))

            def threshold(c):
                for t in range(NT):
                    r = rows(t)
                    c.lag(V.scalar_tensor_tensor(dumps[t % 3][0:r, :], probs[0:r, t, :], S["hi"][0:r, t:t + 1],
                                                 probs[0:r, t, :], ALU.is_lt, ALU.mult))
                    if t >= 1:
                        r = rows(t - 1)
                        c.lag(V.max(top8[0:r, 0, t - 1, :], dumps[(t - 1) % 3][0:r, :]))
                c.link(V.max(top8[0:TAIL, 0, NT - 1, :], dumps[(NT - 1) % 3][0:TAIL, :]))
                vals, sums = top8[:, 0, :, :], top8[:, 1, :, :]
                c.link(V.tensor_tensor(sums[:, :, 0], vals[:, :, 0], S["mhi"], ALU.add))
                for k in range(1, 8):
                    c.link(V.tensor_tensor(sums[:, :, k], sums[:, :, k - 1], vals[:, :, k], ALU.add))
                goal8 = S["goal"].unsqueeze(2).broadcast_to([P, NT, 8])
                c.link(V.tensor_tensor(sums, sums, goal8, ALU.is_ge))
                c.link(V.tensor_scalar(S["open"], sums[:, :, 7], 0.5, None, ALU.is_lt))
                c.link(V.tensor_tensor(sums, sums, vals, ALU.mult))
                c.link(V.tensor_reduce(S["tstar"], sums, AX_X, ALU.max))
                c.link(V.tensor_tensor(S["tstar"], S["tstar"], vals[:, :, 7], ALU.max))
                t8 = S["tstar"].unsqueeze(2).broadcast_to([P, NT, 8])
                c.link(V.tensor_tensor(sums, vals, t8, ALU.is_gt))
                c.link(V.tensor_tensor(sums, sums, vals, ALU.mult))
                c.link(V.tensor_reduce(S["above"], sums, AX_X, ALU.add))
                c.link(V.tensor_tensor(S["above"], S["above"], S["mhi"], ALU.add))
                c.link(V.tensor_tensor(S["allow"], S["goal"], S["above"], ALU.subtract))
                c.link(V.reciprocal(S["f1"], S["tstar"]))
                c.link(V.tensor_tensor(S["allow"], S["allow"], S["f1"], ALU.mult))
                c.link(V.tensor_scalar(S["allow"], S["allow"], 1.0, None, ALU.add))
                c.link(V.tensor_scalar(S["nudge"], S["tstar"], 2.0 ** -30, None, ALU.mult))

            PROBE = NT + 5
            MORE_PAIR = 2 * PROBE + 2 + 8
            PAIR = 2 * (PROBE - SHARED + 2) + 2 + 8

            def search(step):
                ch.link(V.tensor_scalar(S["goal"], S["zsum"], P_NUC, None, ALU.mult))
                ch.link(V.tensor_scalar(S["under"], S["goal"], BELOW, None, ALU.mult))
                ch.link(V.tensor_scalar(S["lo"], S["zsum"], LEAST, None, ALU.mult))
                ch.link(V.tensor_copy(S["mlo"], S["zsum"]))
                ch.link(V.memset(S["hi"], 1.5))
                ch.link(V.memset(S["mhi"], 0.0))
                ch.link(V.tensor_scalar(S["probe"], S["lo"], FIRST_PROBE, 0.75, ALU.mult, ALU.min))
                first = sum(1 + 2 * n for n in PAIRS[:step])
                narrow(ch, first)
                base = ch.counts[dve_step]
                with dve.Fori(0, PAIRS[step]) as i:
                    ch.counts[dve_step] = 0
                    ch.base = i * PAIR + base
                    midpoint(ch)
                    narrow(ch, i * 2 + (first + 1))
                    interpolate(ch)
                    narrow(ch, i * 2 + (first + 2))
                    assert ch.counts[dve_step] == PAIR
                ch.base = None
                ch.counts[dve_step] = base + PAIR * PAIRS[step]
                threshold(ch)
                with dve.If(any_row(ch, S["open"]) > 0):
                    verify = Chain(dve, verify_step[step])
                    recheck(verify, None if step == 0 else sum(1 + 2 * n for n in PAIRS))
                    with dve.If(any_row(verify, S["open"]) > 0):
                        more = Chain(dve, more_step[step])
                        with dve.Fori(0, MORE_PAIRS) as i:
                            more.base = i * MORE_PAIR
                            more.counts[more_step[step]] = 0
                            midpoint(more)
                            narrow(more)
                            interpolate(more)
                            narrow(more)
                            assert more.counts[more_step[step]] == MORE_PAIR
                        more.base = None
                        more.counts[more_step[step]] = MORE_PAIRS * MORE_PAIR
                        threshold(more)
                        recheck(more)
                        with dve.If(any_row(more, S["open"]) > 0):
                            full = Chain(dve, full_step[step])
                            with dve.Fori(0, FULL_PROBES) as i:
                                full.base = i * (PROBE + 2)
                                full.counts[full_step[step]] = 0
                                midpoint(full)
                                narrow(full)
                            full.base = None
                            full.counts[full_step[step]] = FULL_PROBES * (PROBE + 2)
                            threshold(full)
                if step == 1:
                    with dve.Else():
                        show_limit(S["tstar"])

            def recheck(c, shared=None):
                if shared is None:
                    mass_above(c, S["tstar"], S["mass"])
                else:
                    mass_shared(c, S["tstar"], shared)
                c.link(V.tensor_tensor(S["missed"], S["mass"], S["goal"], ALU.is_lt))
                c.link(V.tensor_tensor(S["open"], S["open"], S["missed"], ALU.mult))

            def any_row(c, col):
                c.link(V.tensor_reduce(sq32[:, 0, 0:1], col, AX_X, ALU.max))
                c.link(V.transpose(sq32[:, 1, :], sq32[:, 0, :]))
                c.link(V.tensor_reduce(cols[:, 12:13], sq32[:, 1, :], AX_X, ALU.max))
                for q in range(4):
                    c.link(V.tensor_copy(flag[:, q:q + 1], cols[32 * q:32 * q + 1, 12:13]))
                c.link(V.tensor_reduce(flag[:, 4:5], flag[:, 0:4], AX_X, ALU.max))
                c.link(V.tensor_copy(flag_i[:, 0:1], flag[:, 4:5]))
                return dve.value_load(flag_i[0:1, 0:1], min_val=0, max_val=1)

            def keep(t):
                r = rows(t)
                row, ts = probs[0:r, t, :], S["tstar"][0:r, t:t + 1]
                dve.wait_ge(other_ready, ch.counts.get(masked_ready, 0) + 1)
                ch.link(V.tensor_tensor_scan(order[0:r, :], ones[0:r, :].broadcast_to([r, N]), other[t % 2][0:r, :],
                                             0.0, ALU.add, ALU.subtract))
                ch.link(V.tensor_scalar(late[0:r, :], order[0:r, :], S["allow"][0:r, t:t + 1],
                                        S["nudge"][0:r, t:t + 1], ALU.is_ge, ALU.mult))
                ch.link(V.scalar_tensor_tensor(masked[0:r, :], row, ts, late[0:r, :], ALU.subtract, ALU.is_ge))
                ch.link(V.scalar_tensor_tensor(row, masked[0:r, :], 1.0, row, ALU.mult, ALU.mult,
                                               accum_out=S["kept"][0:r, t:t + 1]))
                ch.tell(V.reciprocal(S["kinv"][0:r, t:t + 1], S["kept"][0:r, t:t + 1]), masked_ready)

            def show_threshold():
                ch.tell(V.tensor_scalar(S["tneg"], S["tstar"], -1.0, None, ALU.mult), threshold_ready)

            def add_attended(t):
                r = rows(t)
                dve.wait_ge(ax_made, NT + t + 1)
                row = y[0:r, t, :]
                ch.tell(V.scalar_tensor_tensor(row, ps[0:r, out_bank(NT + t), 0:D], S["kinv"][0:r, t:t + 1], row,
                                               ALU.mult, ALU.add), ax_added)
                stats_of(row, t, finish=(t == NT - 1))

            project_out(0)
            maxima(0)
            dve.wait_ge(exp_ready, NT)
            search(0)
            show_threshold()
            for t in range(NT):
                keep(t)
            project_out(1)
            maxima(1)
            dve.wait_ge(exp_ready, 2 * NT)
            search(1)
            show_threshold()
            def layer3_input(tiles):
                for t in tiles:
                    r = rows(t)
                    dve.wait_ge(norm_ready, t + 1)
                    ch.link(V.tensor_tensor(y[0:r, t, :], y[0:r, t, :], rowv[0:r, 0, :], ALU.mult))
                    dve.wait_ge(x2_biased, t + 1)
                    ch.link(V.tensor_tensor(x3[0:r, t, :], x3[0:r, t, :], y[0:r, t, :], ALU.add))
                    stats_of(x3[0:r, t, :], t)

            def layer3_values(tiles):
                for t in tiles:
                    r = rows(t)
                    dve.wait_ge(v3_made, t + 1)
                    src, scale = ps[0:r, V3_BANKS[t], 0:D], S["dnode"][0:r, t:t + 1]
                    ch.link(V.tensor_scalar(v_high[0:r, t, :], src, scale, None, ALU.mult))
                    ch.tell(V.scalar_tensor_tensor(v_low[0:r, t, :], src, scale, v_high[0:r, t, :], ALU.mult,
                                                   ALU.subtract), v3_taken)

            for t in range(NT):
                keep(t)
                for g in range(2):
                    if t == GROUPS[g][-1] + 3:
                        finish_stats(g)
                if t == 1:
                    dve.wait_ge(part_added, 4 * NT)
                if t >= 2:
                    add_attended(t - 2)
            dve.wait_ge(vec_in, 48)
            dve.wait_ge(dnode_ready, 1)
            layer3_input(GROUPS[0])
            add_attended(NT - 2)
            add_attended(NT - 1)
            take_turned(3, 0)
            layer3_input(GROUPS[1])
            layer3_values(GROUPS[0])
            layer3_input(GROUPS[2])
            take_turned(3, 1)
            layer3_values(GROUPS[1])
            take_turned(3, 2)
            layer3_values(GROUPS[2])
            for t in range(NT):
                r = rows(t)
                dve.wait_ge(l3_made, t + 1)
                o = xres[0:r, t, :]
                ch.tell(V.scalar_tensor_tensor(o, ps[0:r, L3_BANKS[t % 8], 0:D], S["dnode"][0:r, t:t + 1],
                                               rowv[0:r, 2, :],
                                               ALU.mult, ALU.add), l3_taken)
                ch.tell(V.scalar_tensor_tensor(o, o, 0.0, x3[0:r, t, :], ALU.max, ALU.add), out_ready)


INS = ("x", "adj", "L0_gnn_weight", "L0_gnn_learnable_diag_1", "L0_gnn_bias", "L1_gnn_W_sa", "L1_gnn_a_sa",
       "L1_gnn_W_gcnb", "L1_gnn_b_gcnb", "L1_gnn_Wa", "L1_gnn_ba", "L1_gnn_Wb", "L1_gnn_bb", "L2_gnn_W1",
       "L2_gnn_W2", "L2_gnn_W3", "L2_gnn_U1", "L2_gnn_U2", "L2_gnn_U3", "L2_gnn_gamma", "L2_gnn_beta",
       "L3_gnn_W", "L3_gnn_b")


def kernel(**inputs):
    import numpy as np
    import concourse.bacc as bacc
    from concourse.bass_utils import run_bass_kernel_spmd

    nc = bacc.Bacc("TRN2", target_bir_lowering=False, num_devices=1, dynamic_dma_scratch_size=4096)
    arrays, args = {}, []
    for name in INS:
        a = np.ascontiguousarray(inputs[name])
        arrays[f"in_{name}"] = a
        args.append(nc.dram_tensor(f"in_{name}", a.shape, mybir.dt.from_np(a.dtype), kind="ExternalInput").ap())
    out = nc.dram_tensor("out_rows", inputs["x"].shape, F32, kind="ExternalOutput").ap()
    gnn_stack(nc, *args, out)
    result = run_bass_kernel_spmd(nc, [arrays], core_ids=[0])
    return result.results[0]["out_rows"]
```
